# Optimizing a Trainium2 kernel written in Bass

```python
import numpy as np
import jax
import jax.numpy as jnp

def _softmax(x, axis=-1):
    return jax.nn.softmax(x, axis=axis)

def _gelu(x):
    return jax.nn.gelu(x, approximate=True)

def _silu(x):
    return jax.nn.silu(x)

def _sigmoid(x):
    return jax.nn.sigmoid(x)

def _layernorm(x, axis=-1, eps=1e-05):
    m = jnp.mean(x, axis=axis, keepdims=True)
    v = jnp.var(x, axis=axis, keepdims=True)
    return (x - m) / jnp.sqrt(v + eps)

def _scatter_add(tgt, idx, src, axis=0):
    return tgt.at[idx].add(src)

def _segment_sum(src, seg, n):
    return jax.ops.segment_sum(src, seg, n)
kernel_name = 'mk_conv_seq_d4_conv_nchw512_r4_c5c19c'

def setup_inputs(seed: int=0):
    np.random.seed(seed)
    _w = jnp.asarray

    def _rec_inputs():
        import jax
        import jax.numpy as jnp
        _gk = jax.random.key(seed)
        x = -0.0002928 + 1 * jax.random.normal(jax.random.fold_in(_gk, 1), (2, 128, 16, 16), jnp.float32)
        return x
    x = _rec_inputs()

    def _L0_conv_setup():
        import jax, jax.numpy as jnp
        import numpy as np
        C = 128
        NUM_HEADS = 8
        HEAD_DIM = 16
        GROUPS = 32
        EPS = 1e-05
        key = jax.random.key(seed)
        ks = jax.random.split(key, 7)
        x = jax.random.normal(ks[0], (2, C, 16, 16), dtype=jnp.float32)
        norm_w = jnp.ones((C,), jnp.float32)
        norm_b = jnp.zeros((C,), jnp.float32)
        s1 = 1.0 / np.sqrt(C)
        qkv_w = jax.random.uniform(ks[1], (3 * C, C), jnp.float32, -s1, s1)
        qkv_b = jax.random.uniform(ks[2], (3 * C,), jnp.float32, -s1, s1)
        proj_w = jax.random.uniform(ks[3], (C, C), jnp.float32, -s1, s1)
        proj_b = jax.random.uniform(ks[4], (C,), jnp.float32, -s1, s1)
        return {'x': x, 'norm_w': norm_w, 'norm_b': norm_b, 'qkv_w': qkv_w, 'qkv_b': qkv_b, 'proj_w': proj_w, 'proj_b': proj_b}
    _L0_conv_all = _L0_conv_setup()
    _L0_conv_in = {k: v for k, v in _L0_conv_all.items() if k in ('norm_w', 'norm_b', 'qkv_w', 'qkv_b', 'proj_w', 'proj_b')}
    del _L0_conv_all

    def _L1_conv_setup():
        import jax, jax.numpy as jnp
        import numpy as np
        B, C, H, W = (4, 128, 16, 16)
        IC = C // 8

        def conv1x1(x, w, b):
            return jnp.einsum('oi,bihw->bohw', w, x) + b[None, :, None, None]
        key = jax.random.key(seed)
        ks = jax.random.split(key, 16)
        s_in = 1.0 / np.sqrt(C)
        s_ic = 1.0 / np.sqrt(IC)
        d = {'x': jax.random.normal(ks[0], (B, C, H, W), dtype=jnp.float32), 'wq': jax.random.uniform(ks[1], (IC, C), jnp.float32, -s_in, s_in), 'bq': jnp.zeros((IC,), jnp.float32), 'wk': jax.random.uniform(ks[2], (IC, C), jnp.float32, -s_in, s_in), 'bk': jnp.zeros((IC,), jnp.float32), 'wv': jax.random.uniform(ks[3], (IC, C), jnp.float32, -s_in, s_in), 'bv': jnp.zeros((IC,), jnp.float32), 'w_so': jax.random.uniform(ks[4], (C, IC), jnp.float32, -s_ic, s_ic), 'b_so': jnp.zeros((C,), jnp.float32), 'wcq': jax.random.uniform(ks[5], (C, C), jnp.float32, -s_in, s_in), 'bcq': jnp.zeros((C,), jnp.float32), 'wck': jax.random.uniform(ks[6], (C, C), jnp.float32, -s_in, s_in), 'bck': jnp.zeros((C,), jnp.float32), 'wcv': jax.random.uniform(ks[7], (C, C), jnp.float32, -s_in, s_in), 'bcv': jnp.zeros((C,), jnp.float32), 'gamma': jnp.zeros((1,), jnp.float32), 'beta': jnp.zeros((1,), jnp.float32)}
        return d
    _L1_conv_all = _L1_conv_setup()
    _L1_conv_in = {k: v for k, v in _L1_conv_all.items() if k in ('wq', 'bq', 'wk', 'bk', 'wv', 'bv', 'w_so', 'b_so', 'wcq', 'bcq', 'wck', 'bck', 'wcv', 'bcv', 'gamma', 'beta')}
    del _L1_conv_all

    def _L2_conv_setup():
        import jax, jax.numpy as jnp
        import numpy as np
        C = 128
        GROUPS = 32
        EPS = 1e-06

        def group_norm(x, gamma, beta):
            b, c, h, w = x.shape
            xg = x.reshape(b, GROUPS, c // GROUPS, h, w)
            mu = xg.mean(axis=(2, 3, 4), keepdims=True)
            var = xg.var(axis=(2, 3, 4), keepdims=True)
            xn = (xg - mu) * jax.lax.rsqrt(var + EPS)
            xn = xn.reshape(b, c, h, w)
            return xn * gamma[None, :, None, None] + beta[None, :, None, None]

        def conv1x1(x, w, b):
            return jnp.einsum('bchw,oc->bohw', x, w) + b[None, :, None, None]
        key = jax.random.key(seed)
        ks = jax.random.split(key, 12)
        s = 1.0 / np.sqrt(C)
        return {'x': jax.random.normal(ks[0], (2, C, 16, 16), dtype=jnp.float32), 'gn_gamma': jnp.ones((C,), jnp.float32), 'gn_beta': jnp.zeros((C,), jnp.float32), 'wq': jax.random.normal(ks[1], (C, C), jnp.float32) * s, 'bq': jax.random.normal(ks[2], (C,), jnp.float32) * 0.01, 'wk': jax.random.normal(ks[3], (C, C), jnp.float32) * s, 'bk': jax.random.normal(ks[4], (C,), jnp.float32) * 0.01, 'wv': jax.random.normal(ks[5], (C, C), jnp.float32) * s, 'bv': jax.random.normal(ks[6], (C,), jnp.float32) * 0.01, 'wo': jax.random.normal(ks[7], (C, C), jnp.float32) * s, 'bo': jax.random.normal(ks[8], (C,), jnp.float32) * 0.01}
    _L2_conv_all = _L2_conv_setup()
    _L2_conv_in = {k: v for k, v in _L2_conv_all.items() if k in ('gn_gamma', 'gn_beta', 'wq', 'bq', 'wk', 'bk', 'wv', 'bv', 'wo', 'bo')}
    del _L2_conv_all

    def _L3_conv_setup():
        import jax, jax.numpy as jnp
        import numpy as np
        UP = 2
        DOWN = 2
        NEG_SLOPE = 0.2
        MARGIN = 10
        FLRELU_SCALE = np.float32(2.0 ** 0.5)
        UP_PAD = ((10 + 1) // 2 + UP - 1, 10 // 2)
        DOWN_PAD = ((10 + 1) // 2, 10 // 2)
        _FILT = np.array([0.0, 0.00398, -0.01884, -0.05155, 0.12443, 0.44197, 0.44197, 0.12443, -0.05155, -0.01884, 0.00398, 0.0], dtype=np.float32)
        _FILT = _FILT / _FILT.sum()

        def _fir1d(x, k, up, down, pad0, pad1, axis):
            N, C, H, W = x.shape
            xr = x.reshape(N * C, 1, H, W)
            K = k.shape[0]
            kf = k[::-1].astype(x.dtype)
            if axis == 3:
                w = kf.reshape(1, 1, 1, K)
                lhs_dil = (1, up)
                strides = (1, down)
                padding = ((0, 0), (pad0, pad1 + up - 1))
            else:
                w = kf.reshape(1, 1, K, 1)
                lhs_dil = (up, 1)
                strides = (down, 1)
                padding = ((pad0, pad1 + up - 1), (0, 0))
            y = jax.lax.conv_general_dilated(xr, w, window_strides=strides, padding=padding, lhs_dilation=lhs_dil, dimension_numbers=('NCHW', 'OIHW', 'NCHW'))
            return y.reshape(N, C, y.shape[2], y.shape[3])

        def _sep_upfirdn(x, k, up, down, pad):
            x = _fir1d(x, k, up, down, pad[0], pad[1], axis=3)
            x = _fir1d(x, k, up, down, pad[0], pad[1], axis=2)
            return x
        key = jax.random.key(seed)
        k_in = jax.random.fold_in(key, 0)
        return {'input': jax.random.normal(k_in, (8, 128, 16, 16), dtype=jnp.float32), 'bias': jnp.zeros((128,), dtype=jnp.float32), 'up_filter': jnp.asarray(_FILT), 'down_filter': jnp.asarray(_FILT)}
    _L3_conv_all = _L3_conv_setup()
    _L3_conv_in = {k: v for k, v in _L3_conv_all.items() if k in ('bias', 'up_filter', 'down_filter')}
    del _L3_conv_all
    return {'x': x, 'L0_conv_norm_w': _L0_conv_in['norm_w'], 'L0_conv_norm_b': _L0_conv_in['norm_b'], 'L0_conv_qkv_w': _L0_conv_in['qkv_w'], 'L0_conv_qkv_b': _L0_conv_in['qkv_b'], 'L0_conv_proj_w': _L0_conv_in['proj_w'], 'L0_conv_proj_b': _L0_conv_in['proj_b'], 'L1_conv_wq': _L1_conv_in['wq'], 'L1_conv_bq': _L1_conv_in['bq'], 'L1_conv_wk': _L1_conv_in['wk'], 'L1_conv_bk': _L1_conv_in['bk'], 'L1_conv_wv': _L1_conv_in['wv'], 'L1_conv_bv': _L1_conv_in['bv'], 'L1_conv_w_so': _L1_conv_in['w_so'], 'L1_conv_b_so': _L1_conv_in['b_so'], 'L1_conv_wcq': _L1_conv_in['wcq'], 'L1_conv_bcq': _L1_conv_in['bcq'], 'L1_conv_wck': _L1_conv_in['wck'], 'L1_conv_bck': _L1_conv_in['bck'], 'L1_conv_wcv': _L1_conv_in['wcv'], 'L1_conv_bcv': _L1_conv_in['bcv'], 'L1_conv_gamma': _L1_conv_in['gamma'], 'L1_conv_beta': _L1_conv_in['beta'], 'L2_conv_gn_gamma': _L2_conv_in['gn_gamma'], 'L2_conv_gn_beta': _L2_conv_in['gn_beta'], 'L2_conv_wq': _L2_conv_in['wq'], 'L2_conv_bq': _L2_conv_in['bq'], 'L2_conv_wk': _L2_conv_in['wk'], 'L2_conv_bk': _L2_conv_in['bk'], 'L2_conv_wv': _L2_conv_in['wv'], 'L2_conv_bv': _L2_conv_in['bv'], 'L2_conv_wo': _L2_conv_in['wo'], 'L2_conv_bo': _L2_conv_in['bo'], 'L3_conv_bias': _L3_conv_in['bias'], 'L3_conv_up_filter': _L3_conv_in['up_filter'], 'L3_conv_down_filter': _L3_conv_in['down_filter']}

def reference(x, L0_conv_norm_w, L0_conv_norm_b, L0_conv_qkv_w, L0_conv_qkv_b, L0_conv_proj_w, L0_conv_proj_b, L1_conv_wq, L1_conv_bq, L1_conv_wk, L1_conv_bk, L1_conv_wv, L1_conv_bv, L1_conv_w_so, L1_conv_b_so, L1_conv_wcq, L1_conv_bcq, L1_conv_wck, L1_conv_bck, L1_conv_wcv, L1_conv_bcv, L1_conv_gamma, L1_conv_beta, L2_conv_gn_gamma, L2_conv_gn_beta, L2_conv_wq, L2_conv_bq, L2_conv_wk, L2_conv_bk, L2_conv_wv, L2_conv_bv, L2_conv_wo, L2_conv_bo, L3_conv_bias, L3_conv_up_filter, L3_conv_down_filter):
    import jax
    import jax.numpy as jnp

    def _L0_conv_ref(x, norm_w, norm_b, qkv_w, qkv_b, proj_w, proj_b):
        import jax, jax.numpy as jnp
        import numpy as np
        C = 128
        NUM_HEADS = 8
        HEAD_DIM = 16
        GROUPS = 32
        EPS = 1e-05
        b, c, h, w = x.shape
        n = h * w
        x_flat = x.reshape(b, c, n)
        xg = x_flat.reshape(b, GROUPS, c // GROUPS, n)
        mean = xg.mean(axis=(2, 3), keepdims=True)
        var = xg.var(axis=(2, 3), keepdims=True)
        hn = ((xg - mean) * jax.lax.rsqrt(var + EPS)).reshape(b, c, n)
        hn = hn * norm_w[None, :, None] + norm_b[None, :, None]
        qkv = jnp.einsum('oc,bcn->bon', qkv_w, hn) + qkv_b[None, :, None]
        q, k, v = jnp.split(qkv, 3, axis=1)
        q = q.reshape(b, NUM_HEADS, HEAD_DIM, n)
        k = k.reshape(b, NUM_HEADS, HEAD_DIM, n)
        v = v.reshape(b, NUM_HEADS, HEAD_DIM, n)
        scale = HEAD_DIM ** (-0.5)
        attn = jnp.einsum('bhdn,bhdm->bhnm', q, k) * scale
        attn = jax.nn.softmax(attn, axis=-1)
        out = jnp.einsum('bhnm,bhdm->bhdn', attn, v).reshape(b, c, n)
        out = jnp.einsum('oc,bcn->bon', proj_w, out) + proj_b[None, :, None]
        return (x_flat + out).reshape(b, c, h, w)

    def _L1_conv_ref(x, wq, bq, wk, bk, wv, bv, w_so, b_so, wcq, bcq, wck, bck, wcv, bcv, gamma, beta):
        import jax, jax.numpy as jnp
        import numpy as np
        B, C, H, W = (4, 128, 16, 16)
        IC = C // 8

        def conv1x1(x, w, b):
            return jnp.einsum('oi,bihw->bohw', w, x) + b[None, :, None, None]
        b, c, h, w = x.shape
        n = h * w
        q = conv1x1(x, wq, bq).reshape(b, IC, n)
        k = conv1x1(x, wk, bk).reshape(b, IC, n)
        v = conv1x1(x, wv, bv).reshape(b, IC, n)
        energy = jnp.einsum('bcn,bcm->bnm', q, k)
        attn = jax.nn.softmax(energy, axis=-1)
        out_s = jnp.einsum('bcn,bmn->bcm', v, attn)
        out_s = out_s.reshape(b, IC, h, w)
        out_s = conv1x1(out_s, w_so, b_so)
        F_s = gamma * out_s + x
        qc = conv1x1(x, wcq, bcq).reshape(b, c, n)
        kc = conv1x1(x, wck, bck).reshape(b, c, n)
        vc = conv1x1(x, wcv, bcv).reshape(b, c, n)
        energy_c = jnp.einsum('bcn,bdn->bcd', qc, kc)
        attn_c = jax.nn.softmax(energy_c, axis=-1)
        out_c = jnp.einsum('bcd,bdn->bcn', attn_c, vc).reshape(b, c, h, w)
        F_c = beta * out_c + x
        return F_s + F_c

    def _L2_conv_ref(x, gn_gamma, gn_beta, wq, bq, wk, bk, wv, bv, wo, bo):
        import jax, jax.numpy as jnp
        import numpy as np
        C = 128
        GROUPS = 32
        EPS = 1e-06

        def group_norm(x, gamma, beta):
            b, c, h, w = x.shape
            xg = x.reshape(b, GROUPS, c // GROUPS, h, w)
            mu = xg.mean(axis=(2, 3, 4), keepdims=True)
            var = xg.var(axis=(2, 3, 4), keepdims=True)
            xn = (xg - mu) * jax.lax.rsqrt(var + EPS)
            xn = xn.reshape(b, c, h, w)
            return xn * gamma[None, :, None, None] + beta[None, :, None, None]

        def conv1x1(x, w, b):
            return jnp.einsum('bchw,oc->bohw', x, w) + b[None, :, None, None]
        b, c, h, w = x.shape
        hn = group_norm(x, gn_gamma, gn_beta)
        q = conv1x1(hn, wq, bq).reshape(b, c, h * w)
        k = conv1x1(hn, wk, bk).reshape(b, c, h * w)
        v = conv1x1(hn, wv, bv).reshape(b, c, h * w)
        scale = c ** (-0.5)
        scores = jnp.einsum('bci,bcj->bij', q, k) * scale
        attn = jax.nn.softmax(scores, axis=2)
        out = jnp.einsum('bcj,bij->bci', v, attn).reshape(b, c, h, w)
        out = conv1x1(out, wo, bo)
        return x + out

    def _L3_conv_ref(input, bias, up_filter, down_filter):
        import jax, jax.numpy as jnp
        import numpy as np
        UP = 2
        DOWN = 2
        NEG_SLOPE = 0.2
        MARGIN = 10
        FLRELU_SCALE = np.float32(2.0 ** 0.5)
        UP_PAD = ((10 + 1) // 2 + UP - 1, 10 // 2)
        DOWN_PAD = ((10 + 1) // 2, 10 // 2)
        _FILT = np.array([0.0, 0.00398, -0.01884, -0.05155, 0.12443, 0.44197, 0.44197, 0.12443, -0.05155, -0.01884, 0.00398, 0.0], dtype=np.float32)
        _FILT = _FILT / _FILT.sum()

        def _fir1d(x, k, up, down, pad0, pad1, axis):
            N, C, H, W = x.shape
            xr = x.reshape(N * C, 1, H, W)
            K = k.shape[0]
            kf = k[::-1].astype(x.dtype)
            if axis == 3:
                w = kf.reshape(1, 1, 1, K)
                lhs_dil = (1, up)
                strides = (1, down)
                padding = ((0, 0), (pad0, pad1 + up - 1))
            else:
                w = kf.reshape(1, 1, K, 1)
                lhs_dil = (up, 1)
                strides = (down, 1)
                padding = ((pad0, pad1 + up - 1), (0, 0))
            y = jax.lax.conv_general_dilated(xr, w, window_strides=strides, padding=padding, lhs_dilation=lhs_dil, dimension_numbers=('NCHW', 'OIHW', 'NCHW'))
            return y.reshape(N, C, y.shape[2], y.shape[3])

        def _sep_upfirdn(x, k, up, down, pad):
            x = _fir1d(x, k, up, down, pad[0], pad[1], axis=3)
            x = _fir1d(x, k, up, down, pad[0], pad[1], axis=2)
            return x
        out = input + bias[None, :, None, None]
        upf = up_filter * UP
        out = _sep_upfirdn(out, upf, UP, 1, UP_PAD)
        out = jax.nn.leaky_relu(out, NEG_SLOPE) * FLRELU_SCALE
        out = _sep_upfirdn(out, down_filter, 1, DOWN, DOWN_PAD)
        m = (MARGIN * UP - MARGIN * DOWN) // 2
        if m > 0:
            out = out[:, :, m:-m, m:-m]
        return out

    def _gn(v, G=32, eps=1e-05):
        B_, C_, H_, W_ = v.shape
        g = v.reshape(B_, G, C_ // G, H_, W_)
        m = jnp.mean(g, axis=(2, 3, 4), keepdims=True)
        s = jnp.var(g, axis=(2, 3, 4), keepdims=True)
        return ((g - m) / jnp.sqrt(s + eps)).reshape(v.shape)

    def _ln_c(v, eps=1e-06):
        m = jnp.mean(v, axis=1, keepdims=True)
        s = jnp.var(v, axis=1, keepdims=True)
        return (v - m) / jnp.sqrt(s + eps)

    def _ln_t(v, eps=1e-05):
        m = jnp.mean(v, axis=-1, keepdims=True)
        s = jnp.var(v, axis=-1, keepdims=True)
        return (v - m) / jnp.sqrt(s + eps)

    def _to_tokens(v):
        B_, C_, H_, W_ = v.shape
        return v.reshape(B_, C_, H_ * W_).transpose(0, 2, 1)

    def _from_tokens(t, like):
        B_, C_, H_, W_ = like.shape
        return t.transpose(0, 2, 1).reshape(B_, C_, H_, W_)
    x = _L0_conv_ref(x, L0_conv_norm_w, L0_conv_norm_b, L0_conv_qkv_w, L0_conv_qkv_b, L0_conv_proj_w, L0_conv_proj_b)
    x = _L1_conv_ref(x, L1_conv_wq, L1_conv_bq, L1_conv_wk, L1_conv_bk, L1_conv_wv, L1_conv_bv, L1_conv_w_so, L1_conv_b_so, L1_conv_wcq, L1_conv_bcq, L1_conv_wck, L1_conv_bck, L1_conv_wcv, L1_conv_bcv, L1_conv_gamma, L1_conv_beta)
    x = _L2_conv_ref(x, L2_conv_gn_gamma, L2_conv_gn_beta, L2_conv_wq, L2_conv_bq, L2_conv_wk, L2_conv_bk, L2_conv_wv, L2_conv_bv, L2_conv_wo, L2_conv_bo)
    x = _L3_conv_ref(x, L3_conv_bias, L3_conv_up_filter, L3_conv_down_filter)
    return x

_drawn_inputs = setup_inputs


def setup_inputs(seed=0):
    import zlib

    import numpy as np

    out = dict(_drawn_inputs(seed))
    spreads = {'L0_conv_norm_w': (1.0, 0.6),
     'L0_conv_norm_b': (0.0, 0.1),
     'L1_conv_bq': (0.0, 0.1),
     'L1_conv_bk': (0.0, 0.1),
     'L1_conv_bv': (0.0, 0.1),
     'L1_conv_b_so': (0.0, 0.1),
     'L1_conv_bcq': (0.0, 0.1),
     'L1_conv_bck': (0.0, 0.1),
     'L1_conv_bcv': (0.0, 0.1),
     'L2_conv_gn_gamma': (1.0, 0.534),
     'L2_conv_gn_beta': (0.0, 0.1),
     'L3_conv_bias': (0.0, 0.1)}
    factors = {'L2_conv_bq': 57.807, 'L2_conv_bk': 64.0, 'L2_conv_bv': 8.0, 'L2_conv_bo': 8.0}
    for name, (base, spread) in spreads.items():
        noise = np.random.default_rng([zlib.crc32(name.encode()), seed]).standard_normal(out[name].shape)
        drawn = base * np.exp(spread * noise) if base else spread * noise
        out[name] = jnp.asarray(drawn.astype(out[name].dtype))
    for name, factor in factors.items():
        out[name] = (out[name] * factor).astype(out[name].dtype)
    return out
```

```python
from contextlib import ExitStack

import concourse.bass as bass
from concourse import mybir

F32 = mybir.dt.float32
F32R = mybir.dt.float32r
I32 = mybir.dt.int32
ALU = mybir.AluOpType
ACT = mybir.ActivationFunctionType
AX = mybir.AxisListType

C = 128
B = 2
S = 16
N = S * S
NT = N // 128
HEADS, HD = 8, 16
QUAD = 4
GROUPS = B * HEADS // QUAD
COMBOS = 4
IC = C // 8
TAPS = 12
BANDS = 8
PADROWS = 22
PADTOP = 3
EPS0, EPS2 = 1e-5, 1e-6
SLOPE, GAIN = 0.2, 2.0 ** 0.5
SCALE0 = HD ** -0.5
SCALE2 = C ** -0.5
RSQRT_SEED = 1597463007.0

COLS = ("norm_w norm_b qb kb vb pb gn_w gn_b bq bk bv bo bcv b_so gamma beta l3b "
        "q1b k1b q1b_lo k1b_lo q1_lo k1_lo").split()
COL = {name: i for i, name in enumerate(COLS)}

E_AVG, E_ID, E_ID32, E_SHIFT, E_COLS = 0, 128, 256, 288, 290
E_WIDTH = E_COLS + len(COLS)
A_PROJ, A_QK1, A_CQK, A_CV = 0, 128, 256, 512
A_WIDTH = 640
L_Q, L_K, L_V, L_O, L_UR, L_UC, L_DR, L_DC = 0, 128, 256, 384, 512, 516, 548, 556
L_WIDTH = L_DC + S


def build(nc, x_in, early_in, wqkv_in, mid_in, small_in, rows_in, late_in, out):
    with ExitStack() as ctx:
        def sb(name, shape, dt=F32):
            return ctx.enter_context(nc.sbuf_tensor(name, shape, dt))

        def sem(name):
            return ctx.enter_context(nc.semaphore(name))

        bank = [ctx.enter_context(nc.psum_tensor(f"bank{i}", [128, 512], F32)) for i in range(8)]
        PASS1, PASS2, UBANK, TBANK = bank[0:2], bank[4:7], bank[2:4], bank[7]
        K0, K1, K2, K3 = (bank[0], bank[4]), (bank[1], bank[5]), (bank[2], bank[3]), (bank[7], bank[6])

        x = sb("x", [C, B, N])
        early = sb("early", [128, E_WIDTH])
        wqkv = sb("wqkv", [C, 3 * C])
        mid = sb("mid", [C, A_WIDTH])
        small = sb("small", [IC, 2 * C + 1])
        rows = sb("rows", [128, 2 * C])
        late = sb("late", [128, L_WIDTH])
        avg, ident = early[:, E_AVG:E_AVG + 128], early[:, E_ID:E_ID + 128]

        def col(name, n=128):
            i = E_COLS + COL[name]
            return early[0:n, i:i + 1]

        split_sel = sb("split_sel", [C, 4, 4, 128], F32R)
        identr = sb("identr", [128, 128], F32R)
        shift_sel = sb("shift_sel", [128, 2, 128], F32R)
        wfold = sb("wfold", [C, 2, C])
        derived = sb("derived", [C, 8])
        PB, B1, BCV, BQ2, B2, T0, T1 = (derived[:, i:i + 1] for i in range(7))
        upm = sb("upm", [128, 4, 32])

        stat_raw = sb("stat_raw", [C, B, 6])
        stat = sb("stat", [C, B, 2])
        gstat = sb("gstat", [C, B, 2])
        gn = sb("gn", [C, 10, B])
        hn = sb("hn", [C, B, N])
        q_hi, q_lo = sb("q_hi", [C, B, N], F32R), sb("q_lo", [C, B, N], F32R)
        k_hi, k_lo = sb("k_hi", [C, B, N], F32R), sb("k_lo", [C, B, N], F32R)
        qs, ks = sb("qs", [128, 4, B, N], F32R), sb("ks", [128, 4, B, N], F32R)
        vt = sb("vt", [128, B, NT, HEADS, 32])
        negmax = sb("negmax", [128, 2, NT, 2, 2])
        nm = sb("nm", [128, 2, NT, 2, 64], F32R)
        nmt = sb("nmt", [128, 2, N], F32R)
        p0 = sb("p0", [128, 2, NT, 2, 2, N])
        us = sb("us", [128, B, 512])
        rsum = sb("rsum", [128, B, NT * HEADS])
        un = sb("un", [128, B, NT * HEADS, HD])
        oc = sb("oc", [C, B, N])
        xb = sb("xb", [C, B, N])
        x1 = sb("x1", [C, B, N])
        lo1 = sb("lo1", [64, B, 2, N], F32R)
        qk1 = sb("qk1", [64, B, 2, N], F32R)
        cqk = sb("cqk", [128, B, NT, 2 * C])
        v1t = sb("v1t", [128, B, NT, C])
        vc = sb("vc", [C, B, N])
        red1 = sb("red1", [128, B, 3, NT + 1])
        p1 = sb("p1", [128, B, NT, N])
        p1n = sb("p1n", [128, B, NT, N])
        p1t = sb("p1t", [128, B, NT, N])
        pc = sb("pc", [128, B, 2, C])
        pct = sb("pct", [128, B, C])
        x1b = sb("x1b", [C, B, N])
        x2 = sb("x2", [C, B, N])
        stat_raw2 = sb("stat_raw2", [C, B, 6])
        stat2 = sb("stat2", [C, B, 2])
        gstat2 = sb("gstat2", [C, B, 2])
        gn2 = sb("gn2", [C, B, 16])
        hn2 = sb("hn2", [C, B, N])
        q2, k2 = sb("q2", [C, B, N]), sb("k2", [C, B, N])
        v2t = sb("v2t", [128, B, NT, C])
        red2 = sb("red2", [128, B, 3, NT])
        p2 = sb("p2", [128, B, NT, N])
        p2n = sb("p2n", [128, B, NT, N])
        p2t = sb("p2t", [128, B, NT, N])
        x2b = sb("x2b", [C, B, N])
        xpad = sb("xpad", [C, B, PADROWS * S])
        xt = sb("xt", [128, B, BANDS, C])
        sloped = sb("sloped", [128, B, BANDS, C])
        z = sb("z", [128, B, BANDS, C])
        down = sb("down", [128, 128])
        y = sb("y", [C, B, N])

        s = {name: sem(name) for name in (
            "x_in early_in wqkv_in mid_in small_in rows_in late_in out_done "
            "sel_zero sel_made identr_made shift_made nm_zero vt_ones pad_zero xb_made x1b_made x2b_made "
            "dve_chain stat_made gavg_made hn_made q_made k_made v_made fold_made fold_saved derived_made "
            "q_hi_made k_hi_made q_lo_made k_lo_made vt_made tile_made tile_saved_act tile_saved_dve "
            "pass1_made max_made nm_made nmt_made nmt_saved pass2_made exp_made pv_made "
            "us_saved ut_made un_made unt_made oc_saved proj_made x1_made "
            "q1_made k1_made lo1_made qk1_saved cqk_made cqk_saved v1_made v1_saved "
            "s1_made max1_made exp1_made p1n_made p1t_made p1t_saved "
            "e_made maxe_made expe_made pc_made pct_made pct_saved o1_made x2_made "
            "stat2_made gavg2_made hn2_made q2_made k2_made v2_made q2_saved k2_saved v2_saved "
            "s2_made max2_made exp2_made p2n_made p2t_made p2t_saved o2_made x3_made "
            "xt_made xt_saved_act xt_saved_dve up_made sloped_made z_made upm_made down_saved "
            "y_made y_saved").split()}

        block = ctx.enter_context(nc.Block())

        @block.sync
        def _(sp):
            sp.dma_start(x[:, :, :], x_in.rearrange("b c n -> c b n")).then_inc(s["x_in"], 16)
            sp.dma_start(wqkv[:, :], wqkv_in).then_inc(s["wqkv_in"], 16)
            sp.dma_start(small[:, :], small_in).then_inc(s["small_in"], 16)
            sp.dma_start(late[:, :], late_in).then_inc(s["late_in"], 16)
            for b in range(B):
                sp.wait_ge(s["y_saved"], b + 1)
                sp.dma_start(out[b], y[:, b, :]).then_inc(s["out_done"], 16)
            sp.wait_ge(s["out_done"], 16 * B)

        @block.gpsimd
        def _(pool):
            pool.memset(split_sel[:, :, :, :].bitcast(F32), 0.0).then_inc(s["sel_zero"], 1)
            pool.memset(nm[:, :, :, :, :].bitcast(F32), 0.0).then_inc(s["nm_zero"], 1)
            pool.wait_ge(s["early_in"], 16)
            pool.wait_ge(s["sel_zero"], 1)
            pool.wait_ge(s["nm_zero"], 1)
            for p in range(4):
                block32 = early[32 * p:32 * p + 32, E_ID32:E_ID32 + 32].rearrange("p (h d) -> p h d", h=2)
                src = block32.unsqueeze(2).broadcast_to([32, 2, 2, HD])
                for kind, first, step in ((0, 0, 1), (1, 2, 1), (2, 0, 2), (3, 1, 2)):
                    dst = split_sel[32 * p:32 * p + 32, kind, p, :].rearrange(
                        "p (h r d) -> p h r d", h=2, r=COMBOS)[:, :, first:first + step + 1:step, :]
                    pool.tensor_copy(dst, src).then_inc(s["sel_made"], 1)
                pool.wait_ge(s["sel_made"], 4 * p + 4)
            pool.tensor_copy(identr[:, :], ident).then_inc(s["identr_made"], 1)
            pool.tensor_copy(shift_sel[:, :, :], early[:, E_SHIFT:E_SHIFT + 2].unsqueeze(2)
                             .broadcast_to([128, 2, 128])).then_inc(s["shift_made"], 1)
            pool.memset(vt[:, :, :, :, HD:32], 1.0).then_inc(s["vt_ones"], 1)
            pool.memset(xpad[:, :, :], 0.0).then_inc(s["pad_zero"], 1)
            pool.wait_ge(s["x_in"], 16)
            pool.wait_ge(s["derived_made"], 1)
            pool.tensor_scalar(xb[:, :, :], x[:, :, :], PB, None, ALU.add).then_inc(s["xb_made"], 1)
            for b in range(B):
                pool.wait_ge(s["x1_made"], b + 1)
                pool.tensor_scalar(x1b[:, b, :], x1[:, b, :], 2.0, B1, ALU.mult, ALU.add).then_inc(s["x1b_made"], 1)
            for b in range(B):
                pool.wait_ge(s["x2_made"], b + 1)
                pool.tensor_scalar(x2b[:, b, :], x2[:, b, :], B2, None, ALU.add).then_inc(s["x2b_made"], 1)

        @block.tensor
        def _(pe):
            def mm(o, lhsT, rhs, start=True, stop=True):
                return pe.matmul(o, lhsT, rhs, start=start, stop=stop, skip_group_check=True)

            def project0():
                pe.wait_ge(s["early_in"], 16)
                pe.wait_ge(s["stat_made"], 1)
                mm(TBANK[:, 0:2 * B], avg, stat[:, :, :].rearrange("p b k -> p (b k)")).then_inc(s["gavg_made"], 1)
                pe.wait_ge(s["wqkv_in"], 16)
                pe.wait_ge(s["hn_made"], B)
                flat = hn[:, :, :].rearrange("p b n -> p (b n)")
                mm(bank[0][:, :], wqkv[:, 0:C], flat).then_inc(s["q_made"], 1)
                mm(bank[1][:, :], wqkv[:, C:2 * C], flat).then_inc(s["k_made"], 1)
                for t in range(B * NT):
                    last = mm(bank[2][:, t * C:(t + 1) * C], flat[:, t * 128:(t + 1) * 128], wqkv[:, 2 * C:3 * C])
                last.then_inc(s["v_made"], 1)

            def fold():
                pe.wait_ge(s["mid_in"], 16)
                pe.wait_ge(s["small_in"], 16)
                pe.wait_ge(s["late_in"], 16)
                mm(bank[3][:, 0:C], small[:, 0:C], small[:, C:2 * C])
                mm(bank[3][:, C:2 * C], late[:, L_V:L_V + C], late[:, L_O:L_O + C])
                mm(bank[3][:, 256:257], mid[:, A_PROJ:A_PROJ + C], col("vb"))
                mm(bank[3][:, 257:258], small[:, C:2 * C], small[:, 2 * C:2 * C + 1])
                mm(bank[3][:, 258:259], late[:, L_O:L_O + C], col("bv")).then_inc(s["fold_made"], 1)

            def tile(i):
                p, kind = i // 2, 2 * (i % 2)
                hi, lo = (q_hi, q_lo) if kind == 0 else (k_hi, k_lo)
                if i == 0:
                    pe.wait_ge(s["sel_made"], 16)
                if i < 2:
                    pe.wait_ge(s["k_hi_made" if kind else "q_hi_made"], 1)
                if i >= 3:
                    before = i - 3
                    if before in (1, 3):
                        pe.wait_ge(s["tile_saved_dve"], before // 2 + 1)
                    else:
                        pe.wait_ge(s["tile_saved_act"], [1, 0, 2, 0, 3, 4, 5, 6][before])
                o = PASS2[i % 3]
                mm(o[:, :], split_sel[:, kind, p, :], hi[:, :, :].rearrange("p b n -> p (b n)"), True, False)
                if i < 2:
                    pe.wait_ge(s["k_lo_made" if kind else "q_lo_made"], 1)
                mm(o[:, :], split_sel[:, kind + 1, p, :], lo[:, :, :].rearrange("p b n -> p (b n)"),
                   False, True).then_inc(s["tile_made"], 1)

            def pass1(G, u):
                b, g, nt, hh, n = G // 2, G % 2, u // 2, u % 2, 4 * G + u
                if n == 0:
                    pe.wait_ge(s["tile_saved_act"], 2)
                    pe.wait_ge(s["tile_saved_dve"], 2)
                if n == 4:
                    pe.wait_ge(s["tile_saved_act"], 6)
                if n >= 2:
                    pe.wait_ge(s["max_made"], n - 1)
                r = slice(64 * hh, 64 * hh + 64)
                for pp in range(2):
                    last = mm(PASS1[hh][:, pp * N:(pp + 1) * N], qs[r, 2 * g + pp, b, nt * 128:(nt + 1) * 128],
                              ks[r, 2 * g + pp, b, :])
                last.then_inc(s["pass1_made"], 1)

            def shift_rows(G):
                if G == 0:
                    pe.wait_ge(s["identr_made"], 1)
                pe.wait_ge(s["nm_made"], G + 1)
                if G >= 1:
                    pe.wait_ge(s["nmt_saved"], G)
                for nt in range(NT):
                    last = mm(TBANK[:, nt * 128:(nt + 1) * 128], nm[:, G % 2, nt, :, :].rearrange("p h c -> p (h c)"),
                              identr[:, :])
                last.then_inc(s["nmt_made"], 1)

            def pass2(G, v):
                b, g, mt, hh, n = G // 2, G % 2, v // 2, v % 2, 4 * G + v
                if n >= 3:
                    pe.wait_ge(s["exp_made"], n - 2)
                r = slice(64 * hh, 64 * hh + 64)
                for pp in range(2):
                    mm(PASS2[n % 3][:, pp * N:(pp + 1) * N], ks[r, 2 * g + pp, b, mt * 128:(mt + 1) * 128],
                       qs[r, 2 * g + pp, b, :], pp == 0, False)

            def shift(G, v):
                hh, n = v % 2, 4 * G + v
                if n == 0:
                    pe.wait_ge(s["shift_made"], 1)
                if v == 0:
                    pe.wait_ge(s["nmt_saved"], G + 1)
                r = slice(64 * hh, 64 * hh + 64)
                for pp in range(2):
                    last = mm(PASS2[n % 3][:, pp * N:(pp + 1) * N], shift_sel[r, pp, :], nmt[r, G % 2, :], False, pp == 1)
                last.then_inc(s["pass2_made"], 1)

            def values(G, mt):
                b, g = G // 2, G % 2
                if G == 0 and mt == 0:
                    pe.wait_ge(s["vt_ones"], 1)
                    pe.wait_ge(s["vt_made"], 1)
                if G == 2 and mt == 0:
                    pe.wait_ge(s["fold_saved"], 1)
                    pe.wait_ge(s["derived_made"], 1)
                pe.wait_ge(s["exp_made"], 4 * G + 2 * mt + 2)
                for j in range(QUAD):
                    last = mm(UBANK[b][32 * j:32 * j + 32, g * N:(g + 1) * N], vt[:, b, mt, 4 * g + j, :],
                              p0[:, G % 2, mt, j % 2, j // 2, :], mt == 0, mt == NT - 1)
                last.then_inc(s["pv_made"], 1)

            def untangle(b):
                pe.wait_ge(s["us_saved"], b + 1)
                for nt in range(NT):
                    for g in range(2):
                        t = nt * 2 + g
                        last = pe.transpose(UBANK[b][:, t * 128:(t + 1) * 128],
                                            us[:, b, g * N + nt * 128:g * N + (nt + 1) * 128], ident)
                last.then_inc(s["ut_made"], 1)

            def heads_to_rows(b):
                pe.wait_ge(s["un_made"], b + 1)
                for nt in range(NT):
                    last = pe.transpose(UBANK[b][:, nt * 128:(nt + 1) * 128],
                                        un[:, b, nt * HEADS:(nt + 1) * HEADS, :].rearrange("p h d -> p (h d)"), ident)
                last.then_inc(s["unt_made"], 1)

            def project_out(b):
                pe.wait_ge(s["oc_saved"], b + 1)
                mm(UBANK[b][:, N:2 * N], mid[:, A_PROJ:A_PROJ + C], oc[:, b, :]).then_inc(s["proj_made"], 1)

            def queries1(b):
                pe.wait_ge(s["x1_made"], b + 1)
                if b == 0:
                    pe.wait_ge(s["max_made"], 4 * GROUPS)
                else:
                    pe.wait_ge(s["exp_made"], 4 * GROUPS)
                mm(K0[b][0:64, 0:N], mid[:, A_QK1:A_QK1 + 64], x1[:, b, :]).then_inc(s["q1_made"], 1)
                mm(K3[b][0:64, 0:N], mid[:, A_QK1 + 64:A_QK1 + 128], x1[:, b, :]).then_inc(s["k1_made"], 1)

            def channels1(b):
                for nt in range(NT):
                    last = mm(K1[b][:, nt * N:(nt + 1) * N], x1[:, b, nt * 128:(nt + 1) * 128],
                              mid[:, A_CQK:A_CQK + 2 * C])
                last.then_inc(s["cqk_made"], 1)

            def values1(b):
                pe.wait_ge(s["fold_saved"], 1)
                for nt in range(NT):
                    mm(K2[b][:, nt * 128:(nt + 1) * 128], x1[:, b, nt * 128:(nt + 1) * 128], wfold[:, 0, :])
                mm(K2[b][:, N:2 * N], mid[:, A_CV:A_CV + C], x1[:, b, :]).then_inc(s["v1_made"], 1)

            def scores1(b):
                pe.wait_ge(s["qk1_saved"], 2 * b + 2)
                for nt in range(NT):
                    last = mm(K0[b][:, nt * N:(nt + 1) * N], qk1[:, b, 0, nt * 128:(nt + 1) * 128], qk1[:, b, 1, :])
                last.then_inc(s["s1_made"], 1)

            def channel_scores1(b):
                pe.wait_ge(s["cqk_saved"], b + 1)
                for nt in range(NT):
                    last = mm(K3[b][:, 0:C], cqk[:, b, nt, 0:C], cqk[:, b, nt, C:2 * C], nt == 0, nt == NT - 1)
                last.then_inc(s["e_made"], 1)

            def turn_p1(b):
                for nt in range(NT):
                    pe.wait_ge(s["p1n_made"], NT * b + nt + 1)
                    for mt in range(NT):
                        last = pe.transpose(K1[b][:, mt * N + nt * 128:mt * N + (nt + 1) * 128],
                                            p1n[:, b, nt, mt * 128:(mt + 1) * 128], ident)
                last.then_inc(s["p1t_made"], 1)

            def turn_pc(b):
                pe.wait_ge(s["pc_made"], b + 1)
                pe.transpose(K3[b][:, 0:C], pc[:, b, 1, :], ident).then_inc(s["pct_made"], 1)

            def output1(b):
                pe.wait_ge(s["v1_saved"], b + 1)
                pe.wait_ge(s["pct_saved"], b + 1)
                mm(K2[b][:, 0:N], pct[:, b, :], vc[:, b, :], True, False)
                pe.wait_ge(s["p1t_saved"], b + 1)
                for mt in range(NT):
                    last = mm(K2[b][:, 0:N], v1t[:, b, mt, :], p1t[:, b, mt, :], False, mt == NT - 1)
                last.then_inc(s["o1_made"], 1)

            def average2(b):
                pe.wait_ge(s["stat2_made"], b + 1)
                mm(K2[b][:, 0:2], avg, stat2[:, b, :]).then_inc(s["gavg2_made"], 1)

            def project2(b):
                pe.wait_ge(s["hn2_made"], b + 1)
                mm(K0[b][:, 0:N], late[:, L_Q:L_Q + C], hn2[:, b, :]).then_inc(s["q2_made"], 1)
                mm(K1[b][:, 0:N], late[:, L_K:L_K + C], hn2[:, b, :]).then_inc(s["k2_made"], 1)

            def values2(b):
                for nt in range(NT):
                    last = mm(K3[b][:, nt * 128:(nt + 1) * 128], hn2[:, b, nt * 128:(nt + 1) * 128], wfold[:, 1, :])
                last.then_inc(s["v2_made"], 1)

            def scores2(b):
                pe.wait_ge(s["q2_saved"], b + 1)
                pe.wait_ge(s["k2_saved"], b + 1)
                for nt in range(NT):
                    last = mm(K2[b][:, nt * N:(nt + 1) * N], q2[:, b, nt * 128:(nt + 1) * 128], k2[:, b, :])
                last.then_inc(s["s2_made"], 1)

            def turn_p2(b):
                for nt in range(NT):
                    pe.wait_ge(s["p2n_made"], NT * b + nt + 1)
                    for mt in range(NT):
                        last = pe.transpose(K0[b][:, mt * N + nt * 128:mt * N + (nt + 1) * 128],
                                            p2n[:, b, nt, mt * 128:(mt + 1) * 128], ident)
                last.then_inc(s["p2t_made"], 1)

            def output2(b):
                pe.wait_ge(s["v2_saved"], b + 1)
                pe.wait_ge(s["p2t_saved"], b + 1)
                for mt in range(NT):
                    last = mm(K1[b][:, 0:N], v2t[:, b, mt, :], p2t[:, b, mt, :], mt == 0, mt == NT - 1)
                last.then_inc(s["o2_made"], 1)

            def windows3(b):
                pe.wait_ge(s["x3_made"], b + 1)
                for half, o in enumerate((K2[b], K3[b])):
                    for i in range(4):
                        t = 4 * half + i
                        last = pe.transpose(o[:, i * C:(i + 1) * C], xpad[:, b, 32 * t:32 * t + 128], ident)
                    last.then_inc(s["xt_made"], 1)

            def up3(b):
                for half, o in enumerate((K0[b], K1[b])):
                    if half == 0:
                        pe.wait_ge(s["upm_made"], 1)
                        pe.wait_ge(s["xt_saved_act"], b + 1)
                    else:
                        pe.wait_ge(s["xt_saved_dve"], b + 1)
                    mm(o[:, :], upm[:, :, :].rearrange("p y x -> p (y x)"),
                       xt[:, b, 4 * half:4 * half + 4, :].rearrange("p t c -> p (t c)")).then_inc(s["up_made"], 1)

            def down3(b):
                pe.wait_ge(s["down_saved"], 1)
                for t in range(BANDS):
                    if t % 4 == 0:
                        pe.wait_ge(s["z_made"], 2 * b + t // 4 + 1)
                    last = mm(K2[b][:, 32 * t:32 * t + 128], z[:, b, t, :], down[:, :], t == 0, t == BANDS - 1)
                last.then_inc(s["y_made"], 1)

            project0()
            fold()
            for i in range(4):
                tile(i)
            for u in range(4):
                pass1(0, u)
            for i in range(4, 8):
                tile(i)
            for G in range(GROUPS):
                more = G + 1 < GROUPS
                if more:
                    pass1(G + 1, 0)
                if G == 0:
                    pe.wait_ge(s["tile_saved_act"], 6)
                pass2(G, 0)
                pass2(G, 1)
                shift_rows(G)
                if G > 0:
                    values(G - 1, 0)
                    values(G - 1, 1)
                shift(G, 0)
                shift(G, 1)
                if more:
                    pass1(G + 1, 1)
                pass2(G, 2)
                shift(G, 2)
                if more:
                    pass1(G + 1, 2)
                if G == 3:
                    untangle(0)
                pass2(G, 3)
                shift(G, 3)
                if more:
                    pass1(G + 1, 3)
            heads_to_rows(0)
            project_out(0)
            values(3, 0)
            queries1(0)
            values(3, 1)
            channels1(0)
            values1(0)
            untangle(1)
            scores1(0)
            heads_to_rows(1)
            channel_scores1(0)
            project_out(1)
            queries1(1)
            turn_p1(0)
            channels1(1)
            turn_pc(0)
            values1(1)
            output1(0)
            scores1(1)
            channel_scores1(1)
            average2(0)
            turn_p1(1)
            turn_pc(1)
            project2(0)
            values2(0)
            output1(1)
            scores2(0)
            average2(1)
            turn_p2(0)
            project2(1)
            values2(1)
            output2(0)
            scores2(1)
            windows3(0)
            up3(0)
            turn_p2(1)
            output2(1)
            down3(0)
            windows3(1)
            up3(1)
            down3(1)

        @block.scalar
        def _(act):
            act.dma_start(early[:, :], early_in).then_inc(s["early_in"], 16)
            act.dma_start(mid[:, :], mid_in).then_inc(s["mid_in"], 16)
            act.dma_start(rows[:, :], rows_in.partition_broadcast(128)).then_inc(s["rows_in"], 16)

            def halves0():
                act.wait_ge(s["early_in"], 16)
                act.wait_ge(s["q_made"], 1)
                act.activation(q_hi[:, :, :].rearrange("p b n -> p (b n)"), bank[0][:, :], ACT.Identity,
                               bias=col("qb")).then_inc(s["q_hi_made"], 1)
                act.wait_ge(s["k_made"], 1)
                act.activation(k_hi[:, :, :].rearrange("p b n -> p (b n)"), bank[1][:, :], ACT.Identity,
                               bias=col("kb")).then_inc(s["k_hi_made"], 1)
                act.wait_ge(s["v_made"], 1)
                act.activation(vt[:, :, :, :, 0:HD].rearrange("p b t h d -> p (b t h) d"),
                               bank[2][:, :].rearrange("p (h d) -> p h d", d=HD), ACT.Copy).then_inc(s["vt_made"], 1)

            def save_tile(i):
                act.wait_ge(s["tile_made"], i + 1)
                dst = (ks if i % 2 else qs)[:, i // 2, :, :].rearrange("p b n -> p (b n)")
                act.activation(dst, PASS2[i % 3][:, :], ACT.Copy).then_inc(s["tile_saved_act"], 1)

            def save_fold():
                act.wait_ge(s["fold_made"], 1)
                act.activation(wfold[:, :, :].rearrange("p k c -> p (k c)"), bank[3][:, 0:2 * C],
                               ACT.Copy).then_inc(s["fold_saved"], 1)

            def save_shift(G):
                act.wait_ge(s["nmt_made"], G + 1)
                if G >= 2:
                    act.wait_ge(s["pass2_made"], 4 * (G - 1))
                act.activation(nmt[:, G % 2, :], TBANK[:, 0:N], ACT.Copy).then_inc(s["nmt_saved"], 1)

            def exp0(G, v):
                act.wait_ge(s["pass2_made"], 4 * G + v + 1)
                if G >= 2:
                    act.wait_ge(s["pv_made"], 2 * (G - 2) + v // 2 + 1)
                act.activation(p0[:, G % 2, v // 2, v % 2, :, :].rearrange("p a n -> p (a n)"),
                               PASS2[(4 * G + v) % 3][:, :], ACT.Exp, scale=SCALE0).then_inc(s["exp_made"], 1)

            def save_oc(b):
                act.wait_ge(s["unt_made"], b + 1)
                act.activation(oc[:, b, :], UBANK[b][:, 0:N], ACT.Copy).then_inc(s["oc_saved"], 1)

            def lows1(b):
                act.wait_ge(s["q1_made"], b + 1)
                act.activation(lo1[:, b, 0, :], K0[b][0:64, 0:N], ACT.Identity, bias=col("q1b_lo", 64),
                               scale=col("q1_lo", 64)).then_inc(s["lo1_made"], 1)
                act.wait_ge(s["k1_made"], b + 1)
                act.activation(lo1[:, b, 1, :], K3[b][0:64, 0:N], ACT.Identity, bias=col("k1b_lo", 64),
                               scale=col("k1_lo", 64)).then_inc(s["lo1_made"], 1)

            def save_v1(b):
                act.wait_ge(s["v1_made"], b + 1)
                act.wait_ge(s["derived_made"], 1)
                act.activation(v1t[:, b, :, :].rearrange("p t c -> p (t c)"), K2[b][:, 0:N], ACT.Copy)
                act.activation(vc[:, b, :], K2[b][:, N:2 * N], ACT.Identity, bias=BCV,
                               scale=col("beta")).then_inc(s["v1_saved"], 1)

            def exp1(b):
                act.wait_ge(s["max1_made"], b + 1)
                for nt in range(NT):
                    act.activation(p1[:, b, nt, :], K0[b][:, nt * N:(nt + 1) * N], ACT.Exp,
                                   bias=red1[:, b, 0, nt:nt + 1],
                                   accum_out=red1[:, b, 1, nt:nt + 1]).then_inc(s["exp1_made"], 1)

            def exp_channels1(b):
                act.wait_ge(s["maxe_made"], b + 1)
                act.activation(pc[:, b, 0, :], K3[b][:, 0:C], ACT.Exp, bias=red1[:, b, 0, NT:NT + 1],
                               accum_out=red1[:, b, 1, NT:NT + 1]).then_inc(s["expe_made"], 1)

            def save_pct(b):
                act.wait_ge(s["pct_made"], b + 1)
                act.activation(pct[:, b, :], K3[b][:, 0:C], ACT.Copy).then_inc(s["pct_saved"], 1)

            def save_p1t(b):
                act.wait_ge(s["p1t_made"], b + 1)
                act.activation(p1t[:, b, :, :].rearrange("p t n -> p (t n)"), K1[b][:, :],
                               ACT.Copy).then_inc(s["p1t_saved"], 1)

            def save_q2(b):
                act.wait_ge(s["q2_made"], b + 1)
                act.activation(q2[:, b, :], K0[b][:, 0:N], ACT.Identity, bias=BQ2,
                               scale=SCALE2).then_inc(s["q2_saved"], 1)

            def save_v2(b):
                act.wait_ge(s["v2_made"], b + 1)
                act.activation(v2t[:, b, :, :].rearrange("p t c -> p (t c)"), K3[b][:, 0:N],
                               ACT.Copy).then_inc(s["v2_saved"], 1)

            def exp2(b):
                act.wait_ge(s["max2_made"], b + 1)
                for nt in range(NT):
                    act.activation(p2[:, b, nt, :], K2[b][:, nt * N:(nt + 1) * N], ACT.Exp,
                                   bias=red2[:, b, 0, nt:nt + 1],
                                   accum_out=red2[:, b, 1, nt:nt + 1]).then_inc(s["exp2_made"], 1)

            def save_p2t(b):
                act.wait_ge(s["p2t_made"], b + 1)
                act.activation(p2t[:, b, :, :].rearrange("p t n -> p (t n)"), K0[b][:, :],
                               ACT.Copy).then_inc(s["p2t_saved"], 1)

            def save_windows(b):
                act.wait_ge(s["xt_made"], 2 * b + 1)
                act.activation(xt[:, b, 0:4, :].rearrange("p t c -> p (t c)"), K2[b][:, :],
                               ACT.Copy).then_inc(s["xt_saved_act"], 1)

            def slope3(b):
                for half, o in enumerate((K0[b], K1[b])):
                    act.wait_ge(s["up_made"], 2 * b + half + 1)
                    act.activation(sloped[:, b, 4 * half:4 * half + 4, :].rearrange("p t c -> p (t c)"), o[:, :],
                                   ACT.Copy, scale=SLOPE * GAIN).then_inc(s["sloped_made"], 1)

            halves0()
            save_tile(0)
            save_tile(2)
            for i in range(4, 8):
                save_tile(i)
            save_fold()
            for G in range(GROUPS):
                save_shift(G)
                for v in range(4):
                    exp0(G, v)
            save_oc(0)
            lows1(0)
            save_v1(0)
            exp1(0)
            save_oc(1)
            exp_channels1(0)
            lows1(1)
            save_p1t(0)
            save_pct(0)
            save_v1(1)
            exp1(1)
            exp_channels1(1)
            save_q2(0)
            save_p1t(1)
            save_pct(1)
            save_v2(0)
            exp2(0)
            save_q2(1)
            save_p2t(0)
            save_v2(1)
            exp2(1)
            save_windows(0)
            save_p2t(1)
            slope3(0)
            save_windows(1)
            slope3(1)

        @block.vector
        def _(dve):
            done = [0]

            def then(instruction):
                done[0] += 1
                instruction.then_inc(s["dve_chain"], 1)
                dve.wait_ge(s["dve_chain"], done[0])

            def group_norm(gs, eps, w, bias, t, n):
                mean, square = gs[:, :, 0], gs[:, :, 1]
                then(dve.tensor_tensor(t[0], mean, mean, ALU.mult))
                then(dve.scalar_tensor_tensor(out=t[1], in0=square, scalar=eps, in1=t[0],
                                              op0=ALU.add, op1=ALU.subtract))
                then(dve.tensor_scalar(t[2].bitcast(I32), t[1].bitcast(I32), 1, None, ALU.logical_shift_right))
                dve.tensor_scalar(t[3], t[1], -0.5, None, ALU.mult)
                then(dve.tensor_scalar(t[4].bitcast(I32), t[2].bitcast(I32), -1.0, RSQRT_SEED, ALU.mult, ALU.add))
                r = t[4]
                for i in range(3):
                    then(dve.tensor_tensor(t[5], r, r, ALU.mult))
                    then(dve.tensor_tensor(t[6], t[5], t[3], ALU.mult))
                    nxt = t[7] if i % 2 == 0 else t[4]
                    then(dve.scalar_tensor_tensor(out=nxt, in0=t[6], scalar=1.5, in1=r, op0=ALU.add, op1=ALU.mult))
                    r = nxt
                then(dve.tensor_scalar(t[8], r, w, None, ALU.mult))
                then(dve.tensor_tensor(t[5], mean, t[8], ALU.mult))
                then(dve.tensor_scalar(t[9], t[5], -1.0, bias, ALU.mult, ALU.add))

            def norm0():
                dve.wait_ge(s["x_in"], 16)
                for b in range(B):
                    last = dve.bn_stats(stat_raw[:, b, :], x[:, b, :])
                then(last)
                for b in range(B):
                    last = dve.bn_aggr(stat[:, b, :], stat_raw[:, b, :])
                then(last)
                for b in range(B):
                    last = dve.scalar_tensor_tensor(out=stat[:, b, 1:2], in0=stat[:, b, 0:1], scalar=stat[:, b, 0:1],
                                                    in1=stat[:, b, 1:2], op0=ALU.mult, op1=ALU.add)
                last.then_inc(s["stat_made"], 1)
                dve.wait_ge(s["gavg_made"], 1)
                then(dve.tensor_copy(gstat[:, :, :].rearrange("p b k -> p (b k)"), TBANK[:, 0:2 * B]))
                dve.wait_ge(s["early_in"], 16)
                group_norm(gstat, EPS0, col("norm_w"), col("norm_b"), [gn[:, i, :] for i in range(10)], B)
                for b in range(B):
                    dve.tensor_scalar(hn[:, b, :], x[:, b, :], gn[:, 8, b:b + 1], gn[:, 9, b:b + 1],
                                      ALU.mult, ALU.add).then_inc(s["hn_made"], 1)

            def lows0():
                for hi, lo, name, o, ready, made in ((q_hi, q_lo, "qb", bank[0], "q_hi_made", "q_lo_made"),
                                                     (k_hi, k_lo, "kb", bank[1], "k_hi_made", "k_lo_made")):
                    dve.wait_ge(s[ready], 1)
                    dve.scalar_tensor_tensor(out=lo[:, :, :].rearrange("p b n -> p (b n)"), in0=o[:, :],
                                             scalar=col(name), in1=hi[:, :, :].rearrange("p b n -> p (b n)").bitcast(F32),
                                             op0=ALU.add, op1=ALU.subtract).then_inc(s[made], 1)

            def save_tile(i):
                dve.wait_ge(s["tile_made"], i + 1)
                dst = (ks if i % 2 else qs)[:, i // 2, :, :].rearrange("p b n -> p (b n)")
                dve.tensor_copy(dst, PASS2[i % 3][:, :]).then_inc(s["tile_saved_dve"], 1)

            def derive():
                dve.wait_ge(s["fold_saved"], 1)
                dve.tensor_tensor(PB, bank[3][:, 256:257], col("pb"), ALU.add)
                dve.tensor_tensor(T1, bank[3][:, 258:259], col("bo"), ALU.add)
                dve.tensor_tensor(BCV, col("bcv"), col("beta"), ALU.mult)
                dve.tensor_scalar(BQ2, col("bq"), SCALE2, None, ALU.mult)
                then(dve.tensor_tensor(T0, bank[3][:, 257:258], col("b_so"), ALU.add))
                dve.tensor_tensor(B1, T0, col("gamma"), ALU.mult)
                dve.tensor_tensor(B2, T1, col("l3b"), ALU.add).then_inc(s["derived_made"], 1)

            def filters():
                dve.scalar_tensor_tensor(out=upm[:, :, :], in0=late[:, L_UR:L_UR + 4].unsqueeze(2).broadcast_to([128, 4, 32]),
                                         scalar=4.0, in1=late[:, L_UC:L_UC + 32].unsqueeze(1).broadcast_to([128, 4, 32]),
                                         op0=ALU.mult, op1=ALU.mult).then_inc(s["upm_made"], 1)
                dve.tensor_tensor(down[:, :].rearrange("p (y x) -> p y x", y=8),
                                  late[:, L_DR:L_DR + 8].unsqueeze(2).broadcast_to([128, 8, S]),
                                  late[:, L_DC:L_DC + S].unsqueeze(1).broadcast_to([128, 8, S]),
                                  ALU.mult).then_inc(s["down_saved"], 1)

            def maxima(G, u):
                nt, hh, n = u // 2, u % 2, 4 * G + u
                dve.wait_ge(s["pass1_made"], n + 1)
                dve.tensor_reduce(negmax[:, G % 2, nt, hh, :], PASS1[hh][:, :].rearrange("p (a m) -> p a m", a=2),
                                  AX.X, ALU.max, negate=True).then_inc(s["max_made"], 1)

            def halve_maxima(G):
                if G == 0:
                    dve.wait_ge(s["nm_zero"], 1)
                if G >= 2:
                    dve.wait_ge(s["nmt_made"], G - 1)
                dve.wait_ge(s["max_made"], 4 * G + 4)
                raw = negmax[:, G % 2, :, :, :]
                for nt in range(NT):
                    last = dve.tensor_copy(nm[:, G % 2, nt, :, 0:2], raw[:, nt])
                then(last)
                for nt in range(NT):
                    last = dve.tensor_tensor(nm[:, G % 2, nt, :, 2:4], raw[:, nt],
                                             nm[:, G % 2, nt, :, 0:2].bitcast(F32), ALU.subtract)
                last.then_inc(s["nm_made"], 1)

            def save_u(b):
                dve.wait_ge(s["pv_made"], 4 * b + 4)
                dve.tensor_copy(us[:, b, :], UBANK[b][:, :]).then_inc(s["us_saved"], 1)

            def divide(b):
                dve.wait_ge(s["ut_made"], b + 1)
                u = UBANK[b][:, :].rearrange("p (h d) -> p h d", d=32)
                then(dve.reciprocal(rsum[:, b, :], u[:, :, HD]))
                dve.tensor_tensor(un[:, b, :, :], u[:, :, 0:HD],
                                  rsum[:, b, :].unsqueeze(2).broadcast_to([128, NT * HEADS, HD]),
                                  ALU.mult).then_inc(s["un_made"], 1)

            def add_x(b):
                dve.wait_ge(s["xb_made"], 1)
                dve.wait_ge(s["proj_made"], b + 1)
                dve.tensor_tensor(x1[:, b, :], UBANK[b][:, N:2 * N], xb[:, b, :], ALU.add).then_inc(s["x1_made"], 1)

            def split1(b):
                for k, (o, name) in enumerate(((K0[b], "q1b"), (K3[b], "k1b"))):
                    dve.wait_ge(s["lo1_made"], 2 * b + k + 1)
                    dve.scalar_tensor_tensor(out=qk1[:, b, k, :], in0=o[0:64, 0:N], scalar=col(name, 64),
                                             in1=lo1[:, b, k, :].bitcast(F32), op0=ALU.add,
                                             op1=ALU.subtract).then_inc(s["qk1_saved"], 1)

            def save_cqk(b):
                dve.wait_ge(s["rows_in"], 16)
                dve.wait_ge(s["cqk_made"], b + 1)
                dve.tensor_tensor(cqk[:, b, :, :], K1[b][:, :].rearrange("p (t c) -> p t c", t=NT),
                                  rows[:, :].unsqueeze(1).broadcast_to([128, NT, 2 * C]),
                                  ALU.add).then_inc(s["cqk_saved"], 1)

            def max1(b):
                dve.wait_ge(s["s1_made"], b + 1)
                dve.tensor_reduce(red1[:, b, 0, 0:NT], K0[b][:, :].rearrange("p (t m) -> p t m", t=NT), AX.X, ALU.max,
                                  negate=True).then_inc(s["max1_made"], 1)

            def max_channels1(b):
                dve.wait_ge(s["e_made"], b + 1)
                dve.tensor_reduce(red1[:, b, 0, NT:NT + 1], K3[b][:, 0:C], AX.X, ALU.max,
                                  negate=True).then_inc(s["maxe_made"], 1)

            def divide1(b):
                for nt in range(NT):
                    dve.wait_ge(s["exp1_made"], NT * b + nt + 1)
                    then(dve.reciprocal(red1[:, b, 2, nt:nt + 1], red1[:, b, 1, nt:nt + 1]))
                    dve.tensor_scalar(p1n[:, b, nt, :], p1[:, b, nt, :], red1[:, b, 2, nt:nt + 1], col("gamma"),
                                      ALU.mult, ALU.mult).then_inc(s["p1n_made"], 1)

            def divide_channels1(b):
                dve.wait_ge(s["expe_made"], b + 1)
                then(dve.reciprocal(red1[:, b, 2, NT:NT + 1], red1[:, b, 1, NT:NT + 1]))
                dve.tensor_scalar(pc[:, b, 1, :], pc[:, b, 0, :], red1[:, b, 2, NT:NT + 1], None,
                                  ALU.mult).then_inc(s["pc_made"], 1)

            def add_x1(b):
                dve.wait_ge(s["x1b_made"], b + 1)
                dve.wait_ge(s["o1_made"], b + 1)
                dve.tensor_tensor(x2[:, b, :], K2[b][:, 0:N], x1b[:, b, :], ALU.add).then_inc(s["x2_made"], 1)
                dve.wait_ge(s["x2_made"], b + 1)

            def stats2(b):
                then(dve.bn_stats(stat_raw2[:, b, :], x2[:, b, :]))
                then(dve.bn_aggr(stat2[:, b, :], stat_raw2[:, b, :]))
                dve.scalar_tensor_tensor(out=stat2[:, b, 1:2], in0=stat2[:, b, 0:1], scalar=stat2[:, b, 0:1],
                                         in1=stat2[:, b, 1:2], op0=ALU.mult, op1=ALU.add).then_inc(s["stat2_made"], 1)

            def norm2(b):
                dve.wait_ge(s["gavg2_made"], b + 1)
                then(dve.tensor_copy(gstat2[:, b, :], K2[b][:, 0:2]))
                t = [gn2[:, b, i:i + 1] for i in range(10)]
                group_norm(gstat2[:, b:b + 1, :], EPS2, col("gn_w"), col("gn_b"), t, 1)
                dve.tensor_scalar(hn2[:, b, :], x2[:, b, :], t[8], t[9], ALU.mult, ALU.add).then_inc(s["hn2_made"], 1)

            def save_k2(b):
                dve.wait_ge(s["k2_made"], b + 1)
                dve.tensor_scalar(k2[:, b, :], K1[b][:, 0:N], col("bk"), None, ALU.add).then_inc(s["k2_saved"], 1)

            def max2(b):
                dve.wait_ge(s["s2_made"], b + 1)
                dve.tensor_reduce(red2[:, b, 0, :], K2[b][:, :].rearrange("p (t m) -> p t m", t=NT), AX.X, ALU.max,
                                  negate=True).then_inc(s["max2_made"], 1)

            def divide2(b):
                for nt in range(NT):
                    dve.wait_ge(s["exp2_made"], NT * b + nt + 1)
                    then(dve.reciprocal(red2[:, b, 2, nt:nt + 1], red2[:, b, 1, nt:nt + 1]))
                    dve.tensor_scalar(p2n[:, b, nt, :], p2[:, b, nt, :], red2[:, b, 2, nt:nt + 1], None,
                                      ALU.mult).then_inc(s["p2n_made"], 1)

            def add_x2(b):
                dve.wait_ge(s["pad_zero"], 1)
                dve.wait_ge(s["x2b_made"], b + 1)
                dve.wait_ge(s["o2_made"], b + 1)
                dve.tensor_tensor(xpad[:, b, PADTOP * S:PADTOP * S + N], K1[b][:, 0:N], x2b[:, b, :],
                                  ALU.add).then_inc(s["x3_made"], 1)

            def save_windows(b):
                dve.wait_ge(s["xt_made"], 2 * b + 2)
                dve.tensor_copy(xt[:, b, 4:8, :].rearrange("p t c -> p (t c)"), K3[b][:, :]).then_inc(s["xt_saved_dve"], 1)

            def relu3(b):
                for half, o in enumerate((K0[b], K1[b])):
                    dve.wait_ge(s["sloped_made"], 2 * b + half + 1)
                    dve.scalar_tensor_tensor(out=z[:, b, 4 * half:4 * half + 4, :].rearrange("p t c -> p (t c)"),
                                             in0=o[:, :], scalar=GAIN,
                                             in1=sloped[:, b, 4 * half:4 * half + 4, :].rearrange("p t c -> p (t c)"),
                                             op0=ALU.mult, op1=ALU.max).then_inc(s["z_made"], 1)

            def save_y(b):
                dve.wait_ge(s["y_made"], b + 1)
                dve.tensor_copy(y[:, b, :], K2[b][:, PADTOP * S:PADTOP * S + N]).then_inc(s["y_saved"], 1)

            norm0()
            lows0()
            save_tile(1)
            save_tile(3)
            for u in range(4):
                maxima(0, u)
            halve_maxima(0)
            derive()
            for G in range(1, GROUPS):
                for u in range(4):
                    maxima(G, u)
                halve_maxima(G)
                if G == 1:
                    dve.wait_ge(s["late_in"], 16)
                    filters()
                if G == 3:
                    save_u(0)
                    divide(0)
            add_x(0)
            save_u(1)
            split1(0)
            divide(1)
            save_cqk(0)
            max1(0)
            max_channels1(0)
            add_x(1)
            divide1(0)
            split1(1)
            divide_channels1(0)
            save_cqk(1)
            max1(1)
            add_x1(0)
            stats2(0)
            max_channels1(1)
            divide1(1)
            divide_channels1(1)
            norm2(0)
            save_k2(0)
            add_x1(1)
            stats2(1)
            max2(0)
            norm2(1)
            divide2(0)
            save_k2(1)
            max2(1)
            add_x2(0)
            divide2(1)
            save_windows(0)
            relu3(0)
            add_x2(1)
            save_windows(1)
            save_y(0)
            relu3(1)
            save_y(1)


def toeplitz(f, offset, rows, row_step, cols, col_step):
    import numpy as np
    at = offset + row_step * np.arange(rows)[:, None] + col_step * np.arange(cols)[None, :]
    padded = np.concatenate([f, np.zeros(1, f.dtype)])
    return padded[np.where((at >= 0) & (at < len(f)), at, len(f))]


def kernel(**inputs):
    import numpy as np
    import concourse.bacc as bacc
    from concourse.bass_utils import run_bass_kernel_spmd

    a = {k: np.ascontiguousarray(v) for k, v in inputs.items()}

    def constant(shape):
        return np.zeros(shape, np.float32)

    cols = constant((128, len(COLS)))

    def put(name, v, rows=slice(0, 128)):
        cols[rows, COL[name]] = v

    put("norm_w", a["L0_conv_norm_w"])
    put("norm_b", a["L0_conv_norm_b"])
    for i, name in enumerate(("qb", "kb", "vb")):
        put(name, a["L0_conv_qkv_b"][i * C:(i + 1) * C])
    put("pb", a["L0_conv_proj_b"])
    put("gn_w", a["L2_conv_gn_gamma"])
    put("gn_b", a["L2_conv_gn_beta"])
    for name in ("bq", "bk", "bv", "bo"):
        put(name, a["L2_conv_" + name])
    put("bcv", a["L1_conv_bcv"])
    put("b_so", a["L1_conv_b_so"])
    put("gamma", a["L1_conv_gamma"][0])
    put("beta", a["L1_conv_beta"][0])
    put("l3b", a["L3_conv_bias"])
    for r in range(COMBOS):
        rows = slice(r * IC, (r + 1) * IC)
        put("q1b", a["L1_conv_bq"], rows)
        put("k1b", a["L1_conv_bk"], rows)
        if r >= 2:
            put("q1b_lo", a["L1_conv_bq"], rows)
            put("q1_lo", 1.0, rows)
        if r % 2:
            put("k1b_lo", a["L1_conv_bk"], rows)
            put("k1_lo", 1.0, rows)

    early = constant((128, E_WIDTH))
    channel = np.arange(128)
    early[:, E_AVG:E_AVG + 128] = (channel[:, None] // 4 == channel[None, :] // 4) * 0.25
    early[:, E_ID:E_ID + 128] = np.eye(128)
    early[:, E_ID32:E_ID32 + 32] = channel[:, None] % 32 == np.arange(32)[None, :]
    for pp in range(2):
        early[:, E_SHIFT + pp] = (channel % 64 == pp) | (channel % 64 == pp + 2)
    early[:, E_COLS:] = cols

    mid = np.concatenate([a["L0_conv_proj_w"].T] + [a["L1_conv_wq"].T] * COMBOS + [a["L1_conv_wk"].T] * COMBOS
                         + [a["L1_conv_wcq"].T, a["L1_conv_wck"].T, a["L1_conv_wcv"].T], 1)
    small = np.concatenate([a["L1_conv_wv"], a["L1_conv_w_so"].T, a["L1_conv_bv"][:, None]], 1)
    rows = np.concatenate([a["L1_conv_bcq"], a["L1_conv_bck"]])
    up, dn = a["L3_conv_up_filter"], a["L3_conv_down_filter"]
    up_rows = np.repeat(toeplitz(up, 11, 8, -2, 4, 1), S, 0)
    up_cols = np.tile(toeplitz(up, 5, S, -2, 32, 1), (8, 1))
    dn_rows = np.repeat(toeplitz(dn, 0, 4, -1, 8, 2), 32, 0)
    dn_cols = np.tile(toeplitz(dn, 6, 32, -1, S, 2), (4, 1))
    late = np.concatenate([a["L2_conv_wq"].T, a["L2_conv_wk"].T, a["L2_conv_wv"], a["L2_conv_wo"].T,
                           up_rows, up_cols, dn_rows, dn_cols], 1)
    arrays = {
        "x": a["x"].reshape(B, C, N), "early": early, "wqkv": np.ascontiguousarray(a["L0_conv_qkv_w"].T),
        "mid": np.ascontiguousarray(mid), "small": np.ascontiguousarray(small), "rows": rows,
        "late": np.ascontiguousarray(late),
    }
    nc = bacc.Bacc("TRN2", target_bir_lowering=False, num_devices=1)
    args = [nc.dram_tensor(f"in_{n}", v.shape, F32, kind="ExternalInput").ap() for n, v in arrays.items()]
    out = nc.dram_tensor("out", (B, C, N), F32, kind="ExternalOutput").ap()
    build(nc, *args, out)
    got = run_bass_kernel_spmd(nc, [{f"in_{n}": v for n, v in arrays.items()}], core_ids=[0])
    return got.results[0]["out"].reshape(B, C, S, S)
```

```python
from contextlib import ExitStack

import concourse.bass as bass
from concourse import mybir

F32 = mybir.dt.float32
F32R = mybir.dt.float32r
I32 = mybir.dt.int32
ALU = mybir.AluOpType
ACT = mybir.ActivationFunctionType
AX = mybir.AxisListType

C = 128
B = 2
S = 16
N = S * S
NT = N // 128
HEADS, HD = 8, 16
QUAD = 4
GROUPS = B * HEADS // QUAD
COMBOS = 4
IC = C // 8
TAPS = 12
BANDS = 8
NEAR = 6
PADTOP = 3
EPS0, EPS2 = 1e-5, 1e-6
WARM = dict(stat=0, norm=9, q1=(0, 0), p1=(0, 0), o1=(0, 0), stat2=(1, 0), norm2=(6, 0), s2=(0, 0), p2=(0, 0),
            o2=(0, 0), up=(0, 3), down=(1, 0))
SLOPE, GAIN = 0.2, 2.0 ** 0.5
UP_GAIN = 4.0
SCALE0 = HD ** -0.5
SCALE2 = C ** -0.5
NORM_STEPS = 7
RSQRT_SEED, RSQRT_FIRST, RSQRT_GAIN = 1595932665.0 - 2.0 ** 30, 2.38924456, 0.703952253

COLS = "norm_w norm_b qb kb vb0 vb1 pb gn_w gn_b bq bk bv bo bcv b_so gamma beta l3b q1b k1b".split()
COL = {name: i for i, name in enumerate(COLS)}

E_AVG, E_ID, E_ID32, E_SHIFT, E_COLS = 0, 128, 256, 288, 292
E_WIDTH = E_COLS + len(COLS)
A_PROJ, A_QK1, A_CQK, A_CV, A_SUM = 0, 256, 512, 768, 896
A_WIDTH = A_SUM + QUAD
L_Q, L_K, L_V, L_O, L_UR = 0, 128, 256, 384, 512
L_UC = L_UR + NT * 4 * NEAR
L_DR = L_UC + 32
L_DC = L_DR + 8
L_WIDTH = L_DC + S


def build(nc, x_in, early_in, wqkv_in, mid_in, small_in, rows_in, late_in, out):
    with ExitStack() as ctx:
        def sb(name, shape, dt=F32):
            return ctx.enter_context(nc.sbuf_tensor(name, shape, dt))

        def sem(name):
            return ctx.enter_context(nc.semaphore(name))

        bank = [ctx.enter_context(nc.psum_tensor(f"bank{i}", [128, 512], F32)) for i in range(8)]
        PASS1, PASS2, UBANK, TBANK = bank[0:2], bank[4:7], bank[2:4], bank[7]
        K0, K1, K2, K3 = (bank[0], bank[4]), (bank[1], bank[5]), (bank[3], bank[2]), (bank[7], bank[6])

        S1, P1 = (K0, K3), (K0, K3)
        S2, P2 = (K2, K0), (K1, K2)
        UP = ((K0[0], K1[0]), (K0[1], K1[1], K0[0], K1[0]))

        def part3(b, i):
            per = BANDS // len(UP[b])
            return slice(per * i, per * (i + 1)), b * len(UP[0]) + i + 1

        x = sb("x", [C, B, N])
        early = sb("early", [128, E_WIDTH])
        wqkv = sb("wqkv", [C, 3 * C])
        mid = sb("mid", [C, A_WIDTH])
        small = sb("small", [IC, 2 * C + 1])
        rows = sb("rows", [128, 2 * C])
        late = sb("late", [128, L_WIDTH])
        avg, ident = early[:, E_AVG:E_AVG + 128], early[:, E_ID:E_ID + 128]

        def col(name, n=128):
            i = E_COLS + COL[name]
            return early[0:n, i:i + 1]

        split_sel = sb("split_sel", [C, 4, 4, 128], F32R)
        identr = sb("identr", [128, 128], F32R)
        shift_sel = sb("shift_sel", [128, 4, 128], F32R)
        wfold = sb("wfold", [C, 2, C])
        derived = sb("derived", [C, 8])
        PB, B1, BCV, BQ2, B2, T0, T1 = (derived[:, i:i + 1] for i in range(7))
        upm = sb("upm", [128, NT, 4 * NEAR, 32])
        idle = sb("idle", [128, 128])
        warmed = sb("warmed", [128, 1])

        stat_raw = sb("stat_raw", [C, B, 6])
        stat = sb("stat", [C, B, 2])
        gn = sb("gn", [C, 8, B])
        hn = sb("hn", [C, B, N])
        q_hi, q_lo = sb("q_hi", [C, B, N], F32R), sb("q_lo", [C, B, N], F32R)
        k_hi, k_lo = sb("k_hi", [C, B, N], F32R), sb("k_lo", [C, B, N], F32R)
        qs, ks = sb("qs", [128, 4, 2, B, N], F32R), sb("ks", [128, 4, B, N], F32R)
        vt = sb("vt", [128, B, NT, HEADS, 32])
        negmax = sb("negmax", [128, 2, NT, 2, 2])
        nm = sb("nm", [128, 2, NT, 2, 64], F32R)
        nmt = sb("nmt", [128, 2, N], F32R)
        p0 = sb("p0", [128, 2, NT, 2, 2, N])
        us = sb("us", [128, B, 2, N])
        rsum = sb("rsum", [128, 2, NT, QUAD])
        un = sb("un", [128, B, 2, N])
        xb = sb("xb", [C, B, N])
        x1 = sb("x1", [C, B, N])
        qk1 = sb("qk1", [C, B, 2, N])
        cqk = sb("cqk", [128, B, NT, 2 * C])
        v1t = sb("v1t", [128, B, NT, C])
        vc = sb("vc", [C, B, N])
        red1 = sb("red1", [128, B, 3, NT + 1])
        p1 = sb("p1", [128, B, NT, N])
        p1n = sb("p1n", [128, B, NT, N])
        p1t = sb("p1t", [128, B, NT, N])
        pc = sb("pc", [128, B, 2, C])
        pct = sb("pct", [128, B, C])
        x1b = sb("x1b", [C, B, N])
        x2 = sb("x2", [C, B, N])
        stat_raw2 = sb("stat_raw2", [C, B, 6])
        stat2 = sb("stat2", [C, B, 2])
        gn2 = sb("gn2", [C, B, 8])
        hn2 = sb("hn2", [C, B, N])
        q2, k2 = sb("q2", [C, B, N]), sb("k2", [C, B, N])
        vx = sb("vx", [128, B, 2, NT, C])
        red2 = sb("red2", [128, B, 3, NT])
        p2 = sb("p2", [128, B, NT, N])
        p2t = sb("p2t", [128, B, NT, N])
        x2b = sb("x2b", [C, B, N])
        x3t = sb("x3t", [128, B, NT, C])
        sloped = sb("sloped", [128, B, BANDS, C])
        z = sb("z", [128, B, BANDS, C])
        down = sb("down", [128, 128])
        y = sb("y", [C, B, N])

        s = {name: sem(name) for name in (
            "x_in early_in wqkv_in mid_in small_in rows_in late_in out_done "
            "idle_made sel_zero sel_made qs_zero identr_made shift_made nm_zero vt_ones xb_made x1b_made x2b_made "
            "dve_chain stat_made gavg_made stat_step norm_made norm_step hn_made q_made k_made v_made fold_made fold_saved derived_made "
            "q_hi_made k_hi_made q_lo_made k_lo_made vt_made q_tile_made k_tile_made q_saved_top q_saved_bottom k_saved_act k_saved_dve "
            "pass1_made max_made nm_made nmt_made nmt_saved pass2_made exp_made pv_made "
            "us_saved sums_made inverse_made spread_made un_made proj_made x1_made "
            "q1_made k1_made q1_saved k1_saved cqk_made cqk_saved v1_made v1_saved "
            "s1_made max1_made exp1_made inverse1_made p1n_made p1t_made p1t_saved_act p1t_saved_dve "
            "e_made maxe_made expe_made pc_made pct_made pct_saved o1_made x2_made "
            "hn2_made q2_made k2_made v2_made q2_saved k2_saved v2_saved "
            "s2_made max2_made exp2_made p2t_made p2t_saved_act p2t_saved_dve o2_made x3_made "
            "up_made sloped_made z_made upm_made down_saved "
            "y_made y_saved").split()}

        block = ctx.enter_context(nc.Block())

        @block.sync
        def _(sp):
            sp.dma_start(x[:, :, :], x_in.rearrange("b c n -> c b n")).then_inc(s["x_in"], 16)
            sp.dma_start(wqkv[:, :], wqkv_in).then_inc(s["wqkv_in"], 16)
            sp.dma_start(small[:, :], small_in).then_inc(s["small_in"], 16)
            sp.dma_start(late[:, :], late_in).then_inc(s["late_in"], 16)
            for b in range(B):
                sp.wait_ge(s["y_saved"], b + 1)
                sp.dma_start(out[b], y[:, b, :]).then_inc(s["out_done"], 16)
            sp.wait_ge(s["out_done"], 16 * B)

        @block.gpsimd
        def _(pool):
            pool.memset(split_sel[:, :, :, :].bitcast(F32), 0.0).then_inc(s["sel_zero"], 1)
            pool.memset(nm[:, :, :, :, :].bitcast(F32), 0.0).then_inc(s["nm_zero"], 1)
            pool.wait_ge(s["early_in"], 16)
            pool.wait_ge(s["sel_zero"], 1)
            pool.wait_ge(s["nm_zero"], 1)
            for p in range(4):
                block32 = early[32 * p:32 * p + 32, E_ID32:E_ID32 + 32].rearrange("p (h d) -> p h d", h=2)
                src = block32.unsqueeze(2).broadcast_to([32, 2, 2, HD])
                for kind, first, step in ((0, 0, 1), (1, 2, 1), (2, 0, 2), (3, 1, 2)):
                    dst = split_sel[32 * p:32 * p + 32, kind, p, :].rearrange(
                        "p (h r d) -> p h r d", h=2, r=COMBOS)[:, :, first:first + step + 1:step, :]
                    pool.tensor_copy(dst, src).then_inc(s["sel_made"], 1)
                pool.wait_ge(s["sel_made"], 4 * p + 4)
            pool.tensor_copy(identr[:, :], ident).then_inc(s["identr_made"], 1)
            pool.wait_ge(s["identr_made"], 1)
            for hh in range(2):
                other = slice(64 * (1 - hh), 64 * (1 - hh) + 64)
                pool.memset(qs[other, :, hh, :, :].bitcast(F32), 0.0).then_inc(s["qs_zero"], 1)
                pool.wait_ge(s["qs_zero"], hh + 1)
            pool.tensor_copy(shift_sel[:, :, :], early[:, E_SHIFT:E_SHIFT + 4].unsqueeze(2)
                             .broadcast_to([128, 4, 128])).then_inc(s["shift_made"], 1)
            pool.memset(vt[:, :, :, :, HD:32], 1.0).then_inc(s["vt_ones"], 1)
            pool.wait_ge(s["x_in"], 16)
            pool.wait_ge(s["derived_made"], 1)
            pool.tensor_scalar(xb[:, :, :], x[:, :, :], PB, None, ALU.add).then_inc(s["xb_made"], 1)
            pool.wait_ge(s["late_in"], 16)
            for nt in range(NT):
                taps = late[:, L_UR + nt * 4 * NEAR:L_UR + (nt + 1) * 4 * NEAR]
                pool.tensor_tensor(upm[:, nt, :, :], taps.unsqueeze(2).broadcast_to([128, 4 * NEAR, 32]),
                                   late[:, L_UC:L_UC + 32].unsqueeze(1).broadcast_to([128, 4 * NEAR, 32]),
                                   ALU.mult).then_inc(s["upm_made"], 1)
            for b in range(B):
                pool.wait_ge(s["x1_made"], b + 1)
                pool.tensor_scalar(x1b[:, b, :], x1[:, b, :], 2.0, B1, ALU.mult, ALU.add).then_inc(s["x1b_made"], 1)
            for b in range(B):
                pool.wait_ge(s["x2_made"], b + 1)
                pool.tensor_scalar(x2b[:, b, :], x2[:, b, :], B2, None, ALU.add).then_inc(s["x2b_made"], 1)

        @block.tensor
        def _(pe):
            def mm(o, lhsT, rhs, start=True, stop=True):
                return pe.matmul(o, lhsT, rhs, start=start, stop=stop, skip_group_check=True)

            def warm(n, o=bank[3][:, 0:128]):
                for _ in range(n):
                    mm(o, idle[:, :], idle[:, :])

            def project0():
                pe.wait_ge(s["idle_made"], 1)
                warm(WARM["stat"])
                pe.wait_ge(s["early_in"], 16)
                pe.wait_ge(s["stat_made"], 1)
                mm(TBANK[:, 0:2 * B], avg, stat[:, :, :].rearrange("p b c -> p (b c)")).then_inc(s["gavg_made"], 1)
                warm(WARM["norm"])
                pe.wait_ge(s["wqkv_in"], 16)
                pe.wait_ge(s["hn_made"], B)
                flat = hn[:, :, :].rearrange("p b n -> p (b n)")
                mm(bank[0][:, :], wqkv[:, 0:C], flat).then_inc(s["q_made"], 1)
                mm(bank[1][:, :], wqkv[:, C:2 * C], flat).then_inc(s["k_made"], 1)
                for t in range(B * NT):
                    last = mm(bank[2][:, t * C:(t + 1) * C], flat[:, t * 128:(t + 1) * 128], wqkv[:, 2 * C:3 * C])
                last.then_inc(s["v_made"], 1)

            def fold():
                pe.wait_ge(s["mid_in"], 16)
                pe.wait_ge(s["small_in"], 16)
                pe.wait_ge(s["late_in"], 16)
                mm(bank[3][:, 0:C], small[:, 0:C], small[:, C:2 * C])
                mm(bank[3][:, C:2 * C], late[:, L_V:L_V + C], late[:, L_O:L_O + C])
                for g in range(2):
                    mm(bank[3][:, 256:257], mid[:, A_PROJ + g * C:A_PROJ + (g + 1) * C], col(f"vb{g}"), g == 0, g == 1)
                mm(bank[3][:, 257:258], small[:, C:2 * C], small[:, 2 * C:2 * C + 1])
                mm(bank[3][:, 258:259], late[:, L_O:L_O + C], col("bv")).then_inc(s["fold_made"], 1)

            def wait_k(p):
                pe.wait_ge(s["k_saved_dve"], 1)
                if p > 0:
                    pe.wait_ge(s["k_saved_act"], p)

            def tile(i):
                p, kind = i // 2, 2 * (i % 2)
                hi, lo = (q_hi, q_lo) if kind == 0 else (k_hi, k_lo)
                if i == 0:
                    pe.wait_ge(s["sel_made"], 16)
                if i < 2:
                    pe.wait_ge(s["k_hi_made" if kind else "q_hi_made"], 1)
                if i >= 4:
                    if i % 2:
                        wait_k(p - 2)
                    else:
                        pe.wait_ge(s["q_saved_top"], p - 1)
                        pe.wait_ge(s["q_saved_bottom"], p - 1)
                o = bank[4 + i % 4]
                mm(o[:, :], split_sel[:, kind, p, :], hi[:, :, :].rearrange("p b n -> p (b n)"), True, False)
                if i < 2:
                    pe.wait_ge(s["k_lo_made" if kind else "q_lo_made"], 1)
                mm(o[:, :], split_sel[:, kind + 1, p, :], lo[:, :, :].rearrange("p b n -> p (b n)"),
                   False, True).then_inc(s["k_tile_made" if i % 2 else "q_tile_made"], 1)

            def pass1(G, u):
                b, g, nt, pp, n = G // 2, G % 2, u // 2, u % 2, 4 * G + u
                if n == 0:
                    pe.wait_ge(s["qs_zero"], 2)
                if G < 2 and nt == 0:
                    pe.wait_ge(s["q_saved_top"], 2 * g + pp + 1)
                    pe.wait_ge(s["q_saved_bottom"], 2 * g + pp + 1)
                    wait_k(2 * g + pp)
                if n >= 2:
                    pe.wait_ge(s["max_made"], n - 1)
                for hh in range(2):
                    last = mm(PASS1[pp][:, hh * N:(hh + 1) * N], qs[:, 2 * g + pp, hh, b, nt * 128:(nt + 1) * 128],
                              ks[:, 2 * g + pp, b, :])
                last.then_inc(s["pass1_made"], 1)

            def shift_rows(G):
                if G == 0:
                    pe.wait_ge(s["identr_made"], 1)
                    wait_k(3)
                pe.wait_ge(s["nm_made"], G + 1)
                if G >= 1:
                    pe.wait_ge(s["nmt_saved"], G)
                for nt in range(NT):
                    last = mm(TBANK[:, nt * 128:(nt + 1) * 128], nm[:, G % 2, nt, :, :].rearrange("p h c -> p (h c)"),
                              identr[:, :])
                last.then_inc(s["nmt_made"], 1)

            def pass2(G, v):
                b, g, mt, pp, n = G // 2, G % 2, v // 2, v % 2, 4 * G + v
                if n >= 3:
                    pe.wait_ge(s["exp_made"], n - 2)
                mm(PASS2[n % 3][:, :].rearrange("p (h n) -> p h n", h=2), ks[:, 2 * g + pp, b, mt * 128:(mt + 1) * 128],
                   qs[:, 2 * g + pp, :, b, :], True, False)

            def shift(G, v):
                pp, n = v % 2, 4 * G + v
                if n == 0:
                    pe.wait_ge(s["shift_made"], 1)
                if v == 0:
                    pe.wait_ge(s["nmt_saved"], G + 1)
                for hh in range(2):
                    last = mm(PASS2[n % 3][:, hh * N:(hh + 1) * N], shift_sel[:, 2 * pp + hh, :], nmt[:, G % 2, :],
                              False, hh == 1)
                last.then_inc(s["pass2_made"], 1)

            def values(G, mt):
                b, g = G // 2, G % 2
                if G == 0 and mt == 0:
                    pe.wait_ge(s["vt_ones"], 1)
                    pe.wait_ge(s["vt_made"], 1)
                if G == 1 and mt == 0:
                    pe.wait_ge(s["fold_saved"], 1)
                    pe.wait_ge(s["derived_made"], 1)
                if G == 2 and mt == 0:
                    pe.wait_ge(s["un_made"], 1)
                if G == 3 and mt == 0:
                    pe.wait_ge(s["x1_made"], 1)
                pe.wait_ge(s["exp_made"], 4 * G + 2 * mt + 2)
                for j in range(QUAD):
                    last = mm(UBANK[g][32 * j:32 * j + 32, 0:N], vt[:, b, mt, 4 * g + j, :],
                              p0[:, G % 2, mt, j // 2, j % 2, :], mt == 0, mt == NT - 1)
                last.then_inc(s["pv_made"], 1)

            def sums(G):
                b, g = G // 2, G % 2
                pe.wait_ge(s["us_saved"], G + 1)
                for nt in range(NT):
                    last = mm(UBANK[g][:, N + nt * QUAD:N + (nt + 1) * QUAD], us[:, b, g, nt * 128:(nt + 1) * 128],
                              mid[:, A_SUM:A_SUM + QUAD])
                last.then_inc(s["sums_made"], 1)

            def spread(G):
                g = G % 2
                pe.wait_ge(s["inverse_made"], G + 1)
                for nt in range(NT):
                    for j in range(QUAD):
                        last = mm(UBANK[g][32 * j:32 * j + 32, N + nt * 128:N + (nt + 1) * 128],
                                  rsum[:, g, nt, j:j + 1].broadcast_to([128, 32]), ident)
                last.then_inc(s["spread_made"], 1)

            def project_out(b, g):
                pe.wait_ge(s["un_made"], 3 if (b, g) == (1, 0) else 2 * b + 2)
                last = mm(UBANK[1 - b][:, 0:N], mid[:, A_PROJ + g * C:A_PROJ + (g + 1) * C], un[:, b, g, :], g == 0, g == 1)
                if g == 1:
                    last.then_inc(s["proj_made"], 1)

            def queries1(b):
                if b == 0:
                    pe.wait_ge(s["max_made"], 4 * GROUPS)
                    pe.wait_ge(s["nmt_saved"], GROUPS)
                else:
                    pe.wait_ge(s["exp_made"], 4 * GROUPS)
                warm(WARM["q1"][b], K0[b][:, 0:128])
                pe.wait_ge(s["x1_made"], b + 1)
                mm(K0[b][:, 0:N], mid[:, A_QK1:A_QK1 + C], x1[:, b, :]).then_inc(s["q1_made"], 1)
                mm(K3[b][:, 0:N], mid[:, A_QK1 + C:A_QK1 + 2 * C], x1[:, b, :]).then_inc(s["k1_made"], 1)

            def channels1(b):
                for nt in range(NT):
                    last = mm(K1[b][:, nt * N:(nt + 1) * N], x1[:, b, nt * 128:(nt + 1) * 128],
                              mid[:, A_CQK:A_CQK + 2 * C])
                last.then_inc(s["cqk_made"], 1)

            def values1(b):
                pe.wait_ge(s["fold_saved"], 1)
                if b == 0:
                    pe.wait_ge(s["us_saved"], GROUPS)
                    pe.wait_ge(s["un_made"], GROUPS)
                for nt in range(NT):
                    mm(K2[b][:, nt * 128:(nt + 1) * 128], x1[:, b, nt * 128:(nt + 1) * 128], wfold[:, 0, :])
                mm(K2[b][:, N:2 * N], mid[:, A_CV:A_CV + C], x1[:, b, :]).then_inc(s["v1_made"], 1)

            def scores1(b):
                pe.wait_ge(s["q1_saved"], b + 1)
                pe.wait_ge(s["k1_saved"], b + 1)
                for nt in range(NT):
                    mm(S1[nt][b][:, 0:N], qk1[:, b, 0, nt * 128:(nt + 1) * 128], qk1[:, b, 1, :]).then_inc(s["s1_made"], 1)

            def channel_scores1(b):
                pe.wait_ge(s["cqk_saved"], b + 1)
                for nt in range(NT):
                    last = mm(K1[b][:, 0:C], cqk[:, b, nt, 0:C], cqk[:, b, nt, C:2 * C], nt == 0, nt == NT - 1)
                last.then_inc(s["e_made"], 1)

            def turn_p1(b, nt):
                if nt == 0:
                    warm(WARM["p1"][b], P1[nt][b][:, 0:128])
                pe.wait_ge(s["p1n_made"], NT * b + nt + 1)
                for mt in range(NT):
                    last = pe.transpose(P1[nt][b][:, mt * 128:(mt + 1) * 128],
                                        p1n[:, b, nt, mt * 128:(mt + 1) * 128], ident)
                last.then_inc(s["p1t_made"], 1)

            def turn_pc(b):
                pe.wait_ge(s["pc_made"], b + 1)
                pe.transpose(K1[b][:, 0:C], pc[:, b, 1, :], ident).then_inc(s["pct_made"], 1)

            def output1(b):
                pe.wait_ge(s["v1_saved"], b + 1)
                pe.wait_ge(s["pct_saved"], b + 1)
                mm(K2[b][:, 0:N], pct[:, b, :], vc[:, b, :], True, False)
                warm(WARM["o1"][b], K2[b][:, N:N + 128])
                pe.wait_ge(s["p1t_saved_dve"], b + 1)
                pe.wait_ge(s["p1t_saved_act"], b + 1)
                for mt in range(NT):
                    last = mm(K2[b][:, 0:N], v1t[:, b, mt, :], p1t[:, b, mt, :], False, mt == NT - 1)
                last.then_inc(s["o1_made"], 1)

            def average2(b):
                warm(WARM["stat2"][b], K0[b][:, 0:128])
                pe.wait_ge(s["stat_made"], b + 2)
                mm(K2[b][:, 0:2], avg, stat2[:, b, :]).then_inc(s["gavg_made"], 1)

            def project2(b):
                warm(WARM["norm2"][b], K0[b][:, 0:128])
                pe.wait_ge(s["hn2_made"], b + 1)
                mm(K0[b][:, 0:N], late[:, L_Q:L_Q + C], hn2[:, b, :]).then_inc(s["q2_made"], 1)
                mm(K1[b][:, 0:N], late[:, L_K:L_K + C], hn2[:, b, :]).then_inc(s["k2_made"], 1)

            def values2(b):
                for nt in range(NT):
                    mm(K3[b][:, nt * 128:(nt + 1) * 128], hn2[:, b, nt * 128:(nt + 1) * 128], wfold[:, 1, :])
                pe.wait_ge(s["x2b_made"], b + 1)
                for nt in range(NT):
                    last = pe.transpose(K3[b][:, (NT + nt) * 128:(NT + nt + 1) * 128],
                                        x2b[:, b, nt * 128:(nt + 1) * 128], ident)
                last.then_inc(s["v2_made"], 1)

            def scores2(b):
                warm(WARM["s2"][b], K2[b][:, 0:128])
                pe.wait_ge(s["q2_saved"], b + 1)
                pe.wait_ge(s["k2_saved"], b + 1)
                for nt in range(NT):
                    mm(S2[nt][b][:, 0:N], q2[:, b, nt * 128:(nt + 1) * 128], k2[:, b, :]).then_inc(s["s2_made"], 1)

            def turn_p2(b, nt):
                if nt == 0:
                    warm(WARM["p2"][b], P2[nt][b][:, 0:128])
                pe.wait_ge(s["exp2_made"], NT * b + nt + 1)
                for mt in range(NT):
                    last = pe.transpose(P2[nt][b][:, mt * 128:(mt + 1) * 128],
                                        p2[:, b, nt, mt * 128:(mt + 1) * 128], ident)
                last.then_inc(s["p2t_made"], 1)

            def output2(b):
                pe.wait_ge(s["v2_saved"], b + 1)
                warm(WARM["o2"][b], K3[b][:, 0:128])
                for nt in range(NT):
                    pe.wait_ge(s[("p2t_saved_act", "p2t_saved_dve")[nt]], b + 1)
                    for mt in range(NT):
                        last = mm(K3[b][:, nt * C:(nt + 1) * C], p2t[:, b, nt, mt * 128:(mt + 1) * 128],
                                  vx[:, b, 0, mt, :], mt == 0, mt == NT - 1)
                last.then_inc(s["o2_made"], 1)

            def up3(b):
                pe.wait_ge(s["upm_made"], NT)
                warm(WARM["up"][b], K0[b][:, 0:128])
                for i, o in enumerate(UP[b]):
                    bands, _ = part3(b, i)
                    if i == 2:
                        pe.wait_ge(s["z_made"], len(UP[0]))
                    for t in range(bands.start, bands.stop):
                        tiles = [nt for nt in range(NT) if 0 <= t - 2 * nt < NEAR]
                        for nt in tiles:
                            if t == 2 * nt:
                                pe.wait_ge(s["x3_made"], NT * b + nt + 1)
                            last = mm(o[:, (t - bands.start) * C:(t - bands.start + 1) * C],
                                      upm[:, nt, 4 * (t - 2 * nt):4 * (t - 2 * nt) + 4, :].rearrange("p y x -> p (y x)"),
                                      x3t[:, b, nt, :], nt == tiles[0], nt == tiles[-1])
                    last.then_inc(s["up_made"], 1)

            def down3(b):
                pe.wait_ge(s["down_saved"], 1)
                warm(WARM["down"][b], K2[b][:, 0:128])
                for i in range(len(UP[b])):
                    bands, count = part3(b, i)
                    pe.wait_ge(s["z_made"], count)
                    for t in range(bands.start, bands.stop):
                        last = mm(K2[b][:, 32 * t:32 * t + 128], z[:, b, t, :], down[:, :], t == 0, t == BANDS - 1)
                last.then_inc(s["y_made"], 1)

            project0()
            tile(0)
            tile(1)
            tile(2)
            tile(3)
            fold()
            pass1(0, 0)
            tile(4)
            pass1(0, 1)
            tile(5)
            tile(6)
            pass1(0, 2)
            tile(7)
            pass1(0, 3)
            pe.wait_ge(s["q_saved_top"], 4)
            pe.wait_ge(s["q_saved_bottom"], 4)
            wait_k(3)
            for G in range(GROUPS - 1):
                pass1(G + 1, 0)
                pass2(G, 0)
                pass1(G + 1, 1)
                pass2(G, 1)
                shift_rows(G)
                if G > 0:
                    values(G - 1, 0)
                    values(G - 1, 1)
                shift(G, 0)
                pass1(G + 1, 2)
                shift(G, 1)
                if G > 0:
                    sums(G - 1)
                pass2(G, 2)
                pass1(G + 1, 3)
                shift(G, 2)
                if G > 0:
                    spread(G - 1)
                pass2(G, 3)
                shift(G, 3)
            pass2(3, 0)
            pass2(3, 1)
            project_out(0, 0)
            project_out(0, 1)
            shift_rows(3)
            values(2, 0)
            values(2, 1)
            shift(3, 0)
            shift(3, 1)
            pass2(3, 2)
            sums(2)
            shift(3, 2)
            pass2(3, 3)
            spread(2)
            shift(3, 3)
            queries1(0)
            values(3, 0)
            values(3, 1)
            channels1(0)
            scores1(0)
            sums(3)
            channel_scores1(0)
            spread(3)
            project_out(1, 0)
            project_out(1, 1)
            values1(0)
            queries1(1)
            channels1(1)
            turn_p1(0, 0)
            turn_p1(0, 1)
            turn_pc(0)
            scores1(1)
            output1(0)
            values1(1)
            channel_scores1(1)
            average2(0)
            turn_p1(1, 0)
            turn_p1(1, 1)
            project2(0)
            turn_pc(1)
            values2(0)
            output1(1)
            scores2(0)
            average2(1)
            turn_p2(0, 0)
            turn_p2(0, 1)
            project2(1)
            values2(1)
            output2(0)
            scores2(1)
            up3(0)
            turn_p2(1, 0)
            turn_p2(1, 1)
            down3(0)
            output2(1)
            up3(1)
            down3(1)

        @block.scalar
        def _(act):
            act.dma_start(early[:, :], early_in).then_inc(s["early_in"], 16)
            act.dma_start(mid[:, :], mid_in).then_inc(s["mid_in"], 16)
            act.dma_start(rows[:, :], rows_in.partition_broadcast(128)).then_inc(s["rows_in"], 16)

            act.wait_ge(s["idle_made"], 1)
            act.activation(warmed[:, :], idle[:, 0:1], ACT.Exp)

            def halves0():
                act.wait_ge(s["x_in"], 16)
                act.wait_ge(s["early_in"], 16)
                act.wait_ge(s["norm_made"], 1)
                act.activation(hn[:, 1, :], x[:, 1, :], ACT.Identity, bias=gn[:, 7, 1:2],
                               scale=gn[:, 6, 1:2]).then_inc(s["hn_made"], 1)
                act.wait_ge(s["q_made"], 1)
                act.activation(q_hi[:, :, :].rearrange("p b n -> p (b n)"), bank[0][:, :], ACT.Identity,
                               bias=col("qb")).then_inc(s["q_hi_made"], 1)
                act.wait_ge(s["k_made"], 1)
                act.activation(k_hi[:, :, :].rearrange("p b n -> p (b n)"), bank[1][:, :], ACT.Identity,
                               bias=col("kb")).then_inc(s["k_hi_made"], 1)
                act.wait_ge(s["v_made"], 1)
                act.activation(vt[:, :, :, :, 0:HD].rearrange("p b t h d -> p (b t h) d"),
                               bank[2][:, :].rearrange("p (h d) -> p h d", d=HD), ACT.Copy).then_inc(s["vt_made"], 1)

            def save_q_top(p):
                act.wait_ge(s["q_tile_made"], p + 1)
                act.activation(qs[0:64, p, 0, :, :].rearrange("p b n -> p (b n)"), bank[4 + 2 * p % 4][0:64, :],
                               ACT.Copy).then_inc(s["q_saved_top"], 1)

            def save_k(p):
                act.wait_ge(s["k_tile_made"], p + 1)
                act.activation(ks[:, p, :, :].rearrange("p b n -> p (b n)"), bank[5 + 2 * p % 4][:, :],
                               ACT.Copy).then_inc(s["k_saved_act"], 1)

            def save_fold():
                act.wait_ge(s["fold_made"], 1)
                act.activation(wfold[:, :, :].rearrange("p k c -> p (k c)"), bank[3][:, 0:2 * C],
                               ACT.Copy).then_inc(s["fold_saved"], 1)

            def save_shift(G):
                act.wait_ge(s["nmt_made"], G + 1)
                if G >= 2:
                    act.wait_ge(s["pass2_made"], 4 * (G - 1))
                act.activation(nmt[:, G % 2, :], TBANK[:, 0:N], ACT.Copy).then_inc(s["nmt_saved"], 1)

            def exp0(G, v):
                act.wait_ge(s["pass2_made"], 4 * G + v + 1)
                if G >= 2:
                    act.wait_ge(s["pv_made"], 2 * (G - 2) + v // 2 + 1)
                act.activation(p0[:, G % 2, v // 2, v % 2, :, :].rearrange("p a n -> p (a n)"),
                               PASS2[(4 * G + v) % 3][:, :], ACT.Exp, scale=SCALE0).then_inc(s["exp_made"], 1)

            def save_u(G):
                act.wait_ge(s["pv_made"], 2 * G + 2)
                act.activation(us[:, G // 2, G % 2, :], UBANK[G % 2][:, 0:N], ACT.Copy).then_inc(s["us_saved"], 1)

            def save_q1(b):
                act.wait_ge(s["q1_made"], b + 1)
                act.activation(qk1[:, b, 0, :], K0[b][:, 0:N], ACT.Identity, bias=col("q1b")).then_inc(s["q1_saved"], 1)

            def save_v1(b):
                act.wait_ge(s["v1_made"], b + 1)
                act.wait_ge(s["derived_made"], 1)
                act.activation(v1t[:, b, :, :].rearrange("p t c -> p (t c)"), K2[b][:, 0:N], ACT.Copy)
                act.activation(vc[:, b, :], K2[b][:, N:2 * N], ACT.Identity, bias=BCV,
                               scale=col("beta")).then_inc(s["v1_saved"], 1)

            def exp1(b, nt):
                act.wait_ge(s["max1_made"], NT * b + nt + 1)
                act.activation(p1[:, b, nt, :], S1[nt][b][:, 0:N], ACT.Exp, bias=red1[:, b, 0, nt:nt + 1],
                               accum_out=red1[:, b, 1, nt:nt + 1]).then_inc(s["exp1_made"], 1)

            def exp_channels1(b):
                act.wait_ge(s["maxe_made"], b + 1)
                act.activation(pc[:, b, 0, :], K1[b][:, 0:C], ACT.Exp, bias=red1[:, b, 0, NT:NT + 1],
                               accum_out=red1[:, b, 1, NT:NT + 1]).then_inc(s["expe_made"], 1)

            def save_pct(b):
                act.wait_ge(s["pct_made"], b + 1)
                act.activation(pct[:, b, :], K1[b][:, 0:C], ACT.Copy).then_inc(s["pct_saved"], 1)

            def save_p1t(b):
                act.wait_ge(s["p1t_made"], NT * b + 1)
                act.activation(p1t[:, b, :, 0:128], P1[0][b][:, 0:N].rearrange("p (t n) -> p t n", t=NT),
                               ACT.Copy).then_inc(s["p1t_saved_act"], 1)

            def save_q2(b):
                act.wait_ge(s["q2_made"], b + 1)
                act.activation(q2[:, b, :], K0[b][:, 0:N], ACT.Identity, bias=BQ2,
                               scale=SCALE2).then_inc(s["q2_saved"], 1)

            def save_v2(b):
                act.wait_ge(s["v2_made"], b + 1)
                act.activation(vx[:, b, :, :, :].rearrange("p k t c -> p (k t c)"), K3[b][:, :],
                               ACT.Copy).then_inc(s["v2_saved"], 1)

            def exp2(b, nt):
                act.wait_ge(s["max2_made"], NT * b + nt + 1)
                act.activation(p2[:, b, nt, :], S2[nt][b][:, 0:N], ACT.Exp, bias=red2[:, b, 0, nt:nt + 1],
                               accum_out=red2[:, b, 1, nt:nt + 1]).then_inc(s["exp2_made"], 1)

            def save_p2t(b):
                act.wait_ge(s["p2t_made"], NT * b + 1)
                act.activation(p2t[:, b, 0, :], P2[0][b][:, 0:N], ACT.Copy).then_inc(s["p2t_saved_act"], 1)

            def slope3(b):
                for i, o in enumerate(UP[b]):
                    bands, count = part3(b, i)
                    act.wait_ge(s["up_made"], count)
                    act.activation(sloped[:, b, bands, :].rearrange("p t c -> p (t c)"),
                                   o[:, 0:(bands.stop - bands.start) * C], ACT.Copy, scale=SLOPE).then_inc(s["sloped_made"], 1)

            halves0()
            save_q_top(0)
            save_q_top(1)
            save_k(1)
            for p in range(2, 4):
                save_q_top(p)
                save_k(p)
            save_fold()
            for G in range(GROUPS - 1):
                save_shift(G)
                if G > 0:
                    save_u(G - 1)
                exp0(G, 0)
                exp0(G, 1)
                exp0(G, 2)
                exp0(G, 3)
            save_shift(3)
            save_u(2)
            exp0(3, 0)
            exp0(3, 1)
            exp0(3, 2)
            exp0(3, 3)
            save_q1(0)
            save_u(3)
            exp1(0, 0)
            exp1(0, 1)
            save_v1(0)
            exp_channels1(0)
            save_q1(1)
            save_p1t(0)
            save_pct(0)
            exp1(1, 0)
            exp1(1, 1)
            exp_channels1(1)
            save_v1(1)
            save_pct(1)
            save_p1t(1)
            save_q2(0)
            save_v2(0)
            exp2(0, 0)
            exp2(0, 1)
            save_p2t(0)
            save_q2(1)
            exp2(1, 0)
            exp2(1, 1)
            slope3(0)
            save_v2(1)
            save_p2t(1)
            slope3(1)

        @block.vector
        def _(dve):
            done = [0]

            def then(instruction):
                done[0] += 1
                instruction.then_inc(s["dve_chain"], 1)
                dve.wait_ge(s["dve_chain"], done[0])

            def group_norm(step, averages, w, bias, temps):
                for g, t in zip(averages, temps):
                    if step == 0:
                        last = dve.tensor_scalar(t[0], g[:, 0:1], g[:, 0:1], g[:, 1:2], ALU.mult, ALU.subtract)
                    elif step == 1:
                        last = dve.tensor_scalar(t[1].bitcast(I32), t[0].bitcast(I32), -0.5, RSQRT_SEED,
                                                 ALU.mult, ALU.add)
                    elif step == 2:
                        dve.tensor_scalar(t[2], t[0], 0.5 * RSQRT_GAIN ** 2, None, ALU.mult)
                        last = dve.scalar_tensor_tensor(out=t[3], in0=t[1], scalar=t[1], in1=t[0],
                                                        op0=ALU.mult, op1=ALU.mult)
                    elif step == 3:
                        last = dve.scalar_tensor_tensor(out=t[4], in0=t[3], scalar=RSQRT_FIRST, in1=t[1],
                                                        op0=ALU.add, op1=ALU.mult)
                    elif step == 4:
                        dve.scalar_tensor_tensor(out=t[5], in0=t[4], scalar=t[4], in1=t[2], op0=ALU.mult, op1=ALU.mult)
                        dve.tensor_scalar(t[3], t[4], w, RSQRT_GAIN, ALU.mult, ALU.mult)
                        last = dve.tensor_scalar(t[1], t[4], w, -RSQRT_GAIN, ALU.mult, ALU.mult)
                    elif step == 5:
                        dve.scalar_tensor_tensor(out=t[6], in0=t[5], scalar=1.5, in1=t[3], op0=ALU.add, op1=ALU.mult)
                        last = dve.scalar_tensor_tensor(out=t[0], in0=t[5], scalar=1.5, in1=t[1],
                                                        op0=ALU.add, op1=ALU.mult)
                    else:
                        last = dve.scalar_tensor_tensor(out=t[7], in0=g[:, 0:1], scalar=t[0], in1=bias,
                                                        op0=ALU.mult, op1=ALU.add)
                return last

            def norm0():
                dve.memset(idle[:, :], 0.0).then_inc(s["idle_made"], 1)
                dve.wait_ge(s["x_in"], 16)
                for b in range(B):
                    last = dve.bn_stats(stat_raw[:, b, :], x[:, b, :])
                then(last)
                for b in range(B):
                    last = dve.bn_aggr(stat[:, b, :], stat_raw[:, b, :])
                then(last)
                then(dve.tensor_tensor(gn[:, 0, :], stat[:, :, 0], stat[:, :, 0], ALU.mult))
                dve.scalar_tensor_tensor(out=stat[:, :, 1], in0=gn[:, 0, :], scalar=EPS0, in1=stat[:, :, 1],
                                         op0=ALU.add, op1=ALU.add).then_inc(s["stat_made"], 1)
                dve.wait_ge(s["early_in"], 16)
                dve.wait_ge(s["gavg_made"], 1)
                averages = [TBANK[:, 2 * b:2 * b + 2] for b in range(B)]
                temps = [[gn[:, i, b:b + 1] for i in range(8)] for b in range(B)]
                for step in range(NORM_STEPS):
                    last = group_norm(step, averages, col("norm_w"), col("norm_b"), temps)
                    if step + 1 < NORM_STEPS:
                        then(last)
                last.then_inc(s["norm_made"], 1)
                dve.wait_ge(s["norm_made"], 1)
                dve.tensor_scalar(hn[:, 0, :], x[:, 0, :], gn[:, 6, 0:1], gn[:, 7, 0:1],
                                  ALU.mult, ALU.add).then_inc(s["hn_made"], 1)

            def lows0():
                for hi, lo, name, o, ready, made in ((q_hi, q_lo, "qb", bank[0], "q_hi_made", "q_lo_made"),
                                                     (k_hi, k_lo, "kb", bank[1], "k_hi_made", "k_lo_made")):
                    dve.wait_ge(s[ready], 1)
                    dve.scalar_tensor_tensor(out=lo[:, :, :].rearrange("p b n -> p (b n)"), in0=o[:, :],
                                             scalar=col(name), in1=hi[:, :, :].rearrange("p b n -> p (b n)").bitcast(F32),
                                             op0=ALU.add, op1=ALU.subtract).then_inc(s[made], 1)

            def save_q_bottom(p):
                dve.wait_ge(s["q_tile_made"], p + 1)
                dve.tensor_copy(qs[64:128, p, 1, :, :].rearrange("p b n -> p (b n)"),
                                bank[4 + 2 * p % 4][64:128, :]).then_inc(s["q_saved_bottom"], 1)

            def save_k(p):
                dve.wait_ge(s["k_tile_made"], p + 1)
                dve.tensor_copy(ks[:, p, :, :].rearrange("p b n -> p (b n)"),
                                bank[5 + 2 * p % 4][:, :]).then_inc(s["k_saved_dve"], 1)

            def derive():
                dve.wait_ge(s["fold_saved"], 1)
                dve.tensor_tensor(PB, bank[3][:, 256:257], col("pb"), ALU.add)
                dve.tensor_tensor(T1, bank[3][:, 258:259], col("bo"), ALU.add)
                dve.tensor_tensor(BCV, col("bcv"), col("beta"), ALU.mult)
                dve.tensor_scalar(BQ2, col("bq"), SCALE2, None, ALU.mult)
                then(dve.tensor_tensor(T0, bank[3][:, 257:258], col("b_so"), ALU.add))
                dve.tensor_tensor(B1, T0, col("gamma"), ALU.mult)
                dve.tensor_tensor(B2, T1, col("l3b"), ALU.add).then_inc(s["derived_made"], 1)

            def filters():
                dve.wait_ge(s["late_in"], 16)
                dve.scalar_tensor_tensor(out=down[:, :].rearrange("p (y x) -> p y x", y=8),
                                         in0=late[:, L_DR:L_DR + 8].unsqueeze(2).broadcast_to([128, 8, S]),
                                         scalar=UP_GAIN * GAIN,
                                         in1=late[:, L_DC:L_DC + S].unsqueeze(1).broadcast_to([128, 8, S]),
                                         op0=ALU.mult, op1=ALU.mult).then_inc(s["down_saved"], 1)

            def maxima(G, u):
                nt, pp, n = u // 2, u % 2, 4 * G + u
                dve.wait_ge(s["pass1_made"], n + 1)
                dve.tensor_reduce(negmax[:, G % 2, nt, pp, :], PASS1[pp][:, :].rearrange("p (a m) -> p a m", a=2),
                                  AX.X, ALU.max, negate=True).then_inc(s["max_made"], 1)

            def halve_maxima(G):
                if G == 0:
                    dve.wait_ge(s["nm_zero"], 1)
                if G >= 2:
                    dve.wait_ge(s["nmt_made"], G - 1)
                dve.wait_ge(s["max_made"], 4 * G + 4)
                raw = negmax[:, G % 2, :, :, :].rearrange("p t q h -> p (t q) h")
                halves = nm[:, G % 2, :, :, :].rearrange("p t q c -> p (t q) c")
                then(dve.tensor_copy(halves[:, :, 0:2], raw))
                dve.tensor_tensor(halves[:, :, 2:4], raw, halves[:, :, 0:2].bitcast(F32),
                                  ALU.subtract).then_inc(s["nm_made"], 1)

            def invert(G):
                g = G % 2
                dve.wait_ge(s["sums_made"], G + 1)
                dve.reciprocal(rsum[:, g, :, :].rearrange("p t j -> p (t j)"),
                               UBANK[g][:, N:N + NT * QUAD]).then_inc(s["inverse_made"], 1)

            def divide(G):
                b, g = G // 2, G % 2
                dve.wait_ge(s["us_saved"], G + 1)
                dve.wait_ge(s["spread_made"], G + 1)
                dve.tensor_tensor(un[:, b, g, :], us[:, b, g, :], UBANK[g][:, N:2 * N], ALU.mult).then_inc(s["un_made"], 1)

            def add_x(b):
                dve.wait_ge(s["xb_made"], 1)
                dve.wait_ge(s["proj_made"], b + 1)
                dve.tensor_tensor(x1[:, b, :], UBANK[1 - b][:, 0:N], xb[:, b, :], ALU.add).then_inc(s["x1_made"], 1)

            def save_k1(b):
                dve.wait_ge(s["k1_made"], b + 1)
                dve.tensor_scalar(qk1[:, b, 1, :], K3[b][:, 0:N], col("k1b"), None, ALU.add).then_inc(s["k1_saved"], 1)

            def save_cqk(b):
                dve.wait_ge(s["rows_in"], 16)
                dve.wait_ge(s["cqk_made"], b + 1)
                dve.tensor_tensor(cqk[:, b, :, :], K1[b][:, :].rearrange("p (t c) -> p t c", t=NT),
                                  rows[:, :].unsqueeze(1).broadcast_to([128, NT, 2 * C]),
                                  ALU.add).then_inc(s["cqk_saved"], 1)

            def max1(b, nt):
                dve.wait_ge(s["s1_made"], NT * b + nt + 1)
                dve.tensor_reduce(red1[:, b, 0, nt:nt + 1], S1[nt][b][:, 0:N], AX.X, ALU.max,
                                  negate=True).then_inc(s["max1_made"], 1)

            def max_channels1(b):
                dve.wait_ge(s["e_made"], b + 1)
                dve.tensor_reduce(red1[:, b, 0, NT:NT + 1], K1[b][:, 0:C], AX.X, ALU.max,
                                  negate=True).then_inc(s["maxe_made"], 1)

            def invert1(b, nt):
                dve.wait_ge(s["exp1_made"], NT * b + nt + 1)
                dve.reciprocal(red1[:, b, 2, nt:nt + 1], red1[:, b, 1, nt:nt + 1]).then_inc(s["inverse1_made"], 1)

            def divide1(b, nt):
                dve.wait_ge(s["inverse1_made"], NT * b + nt + 1)
                dve.tensor_scalar(p1n[:, b, nt, :], p1[:, b, nt, :], red1[:, b, 2, nt:nt + 1], col("gamma"),
                                  ALU.mult, ALU.mult).then_inc(s["p1n_made"], 1)

            def divide_channels1(b):
                dve.wait_ge(s["expe_made"], b + 1)
                then(dve.reciprocal(red1[:, b, 2, NT:NT + 1], red1[:, b, 1, NT:NT + 1]))
                dve.tensor_scalar(pc[:, b, 1, :], pc[:, b, 0, :], red1[:, b, 2, NT:NT + 1], None,
                                  ALU.mult).then_inc(s["pc_made"], 1)

            def save_p1t(b):
                dve.wait_ge(s["p1t_made"], NT * b + 2)
                dve.tensor_copy(p1t[:, b, :, 128:256], P1[1][b][:, 0:N].rearrange("p (t n) -> p t n", t=NT)
                                ).then_inc(s["p1t_saved_dve"], 1)

            def add_x1(b):
                dve.wait_ge(s["x1b_made"], b + 1)
                dve.wait_ge(s["o1_made"], b + 1)
                dve.tensor_tensor(x2[:, b, :], K2[b][:, 0:N], x1b[:, b, :], ALU.add).then_inc(s["x2_made"], 1)
                dve.wait_ge(s["x2_made"], b + 1)

            def stats2(b, step):
                if step > 0:
                    dve.wait_ge(s["stat_step"], 3 * b + step)
                if step == 0:
                    last = dve.bn_stats(stat_raw2[:, b, :], x2[:, b, :])
                elif step == 1:
                    last = dve.bn_aggr(stat2[:, b, :], stat_raw2[:, b, :])
                elif step == 2:
                    last = dve.tensor_tensor(gn2[:, b, 0:1], stat2[:, b, 0:1], stat2[:, b, 0:1], ALU.mult)
                else:
                    last = dve.scalar_tensor_tensor(out=stat2[:, b, 1:2], in0=gn2[:, b, 0:1], scalar=EPS2,
                                                    in1=stat2[:, b, 1:2], op0=ALU.add, op1=ALU.add)
                last.then_inc(s["stat_step" if step < 3 else "stat_made"], 1)

            def norm2(b, step):
                if step == 0:
                    dve.wait_ge(s["gavg_made"], b + 2)
                else:
                    dve.wait_ge(s["norm_step"], b * NORM_STEPS + step)
                t = [gn2[:, b, i:i + 1] for i in range(8)]
                if step < NORM_STEPS:
                    group_norm(step, [K2[b][:, 0:2]], col("gn_w"), col("gn_b"), [t]).then_inc(s["norm_step"], 1)
                else:
                    dve.tensor_scalar(hn2[:, b, :], x2[:, b, :], t[6], t[7], ALU.mult, ALU.add).then_inc(s["hn2_made"], 1)

            def save_k2(b):
                dve.wait_ge(s["k2_made"], b + 1)
                dve.tensor_scalar(k2[:, b, :], K1[b][:, 0:N], col("bk"), None, ALU.add).then_inc(s["k2_saved"], 1)

            def max2(b, nt):
                dve.wait_ge(s["s2_made"], NT * b + nt + 1)
                dve.tensor_reduce(red2[:, b, 0, nt:nt + 1], S2[nt][b][:, 0:N], AX.X, ALU.max,
                                  negate=True).then_inc(s["max2_made"], 1)

            def save_p2t(b):
                dve.wait_ge(s["p2t_made"], NT * b + 2)
                dve.tensor_copy(p2t[:, b, 1, :], P2[1][b][:, 0:N]).then_inc(s["p2t_saved_dve"], 1)

            def invert2(b):
                dve.wait_ge(s["exp2_made"], NT * b + 2)
                then(dve.reciprocal(red2[:, b, 2, :], red2[:, b, 1, :]))

            def add_x2(b):
                dve.wait_ge(s["v2_saved"], b + 1)
                dve.wait_ge(s["o2_made"], b + 1)
                for nt in range(NT):
                    dve.scalar_tensor_tensor(out=x3t[:, b, nt, :], in0=K3[b][:, nt * C:(nt + 1) * C],
                                             scalar=red2[:, b, 2, nt:nt + 1], in1=vx[:, b, 1, nt, :],
                                             op0=ALU.mult, op1=ALU.add).then_inc(s["x3_made"], 1)

            def relu3(b):
                for i, o in enumerate(UP[b]):
                    bands, count = part3(b, i)
                    dve.wait_ge(s["sloped_made"], count)
                    dve.tensor_tensor(z[:, b, bands, :].rearrange("p t c -> p (t c)"), o[:, 0:(bands.stop - bands.start) * C],
                                      sloped[:, b, bands, :].rearrange("p t c -> p (t c)"),
                                      ALU.max).then_inc(s["z_made"], 1)

            def save_y(b):
                dve.wait_ge(s["y_made"], b + 1)
                dve.tensor_copy(y[:, b, :], K2[b][:, PADTOP * S:PADTOP * S + N]).then_inc(s["y_saved"], 1)

            norm0()
            lows0()
            save_k(0)
            save_q_bottom(0)
            save_q_bottom(1)
            maxima(0, 0)
            save_q_bottom(2)
            maxima(0, 1)
            save_q_bottom(3)
            maxima(0, 2)
            maxima(0, 3)
            halve_maxima(0)
            derive()
            for G in range(1, GROUPS):
                maxima(G, 0)
                maxima(G, 1)
                if G == 1:
                    filters()
                if G > 1:
                    invert(G - 2)
                maxima(G, 2)
                maxima(G, 3)
                if G > 1:
                    divide(G - 2)
                halve_maxima(G)
            add_x(0)
            invert(2)
            divide(2)
            save_k1(0)
            save_cqk(0)
            invert(3)
            divide(3)
            max1(0, 0)
            max1(0, 1)
            add_x(1)
            invert1(0, 0)
            invert1(0, 1)
            divide1(0, 0)
            max_channels1(0)
            divide1(0, 1)
            save_k1(1)
            divide_channels1(0)
            save_p1t(0)
            max1(1, 0)
            max1(1, 1)
            save_cqk(1)
            add_x1(0)
            stats2(0, 0)
            stats2(0, 1)
            stats2(0, 2)
            stats2(0, 3)
            invert1(1, 0)
            invert1(1, 1)
            divide1(1, 0)
            divide1(1, 1)
            norm2(0, 0)
            norm2(0, 1)
            norm2(0, 2)
            max_channels1(1)
            norm2(0, 3)
            norm2(0, 4)
            norm2(0, 5)
            norm2(0, 6)
            norm2(0, 7)
            save_p1t(1)
            divide_channels1(1)
            save_k2(0)
            add_x1(1)
            stats2(1, 0)
            stats2(1, 1)
            stats2(1, 2)
            stats2(1, 3)
            max2(0, 0)
            max2(0, 1)
            norm2(1, 0)
            norm2(1, 1)
            norm2(1, 2)
            norm2(1, 3)
            norm2(1, 4)
            norm2(1, 5)
            norm2(1, 6)
            norm2(1, 7)
            save_p2t(0)
            invert2(0)
            save_k2(1)
            add_x2(0)
            max2(1, 0)
            max2(1, 1)
            relu3(0)
            save_p2t(1)
            save_y(0)
            invert2(1)
            add_x2(1)
            relu3(1)
            save_y(1)


def toeplitz(f, offset, rows, row_step, cols, col_step):
    import numpy as np
    at = offset + row_step * np.arange(rows)[:, None] + col_step * np.arange(cols)[None, :]
    padded = np.concatenate([f, np.zeros(1, f.dtype)])
    return padded[np.where((at >= 0) & (at < len(f)), at, len(f))]


def kernel(**inputs):
    import numpy as np
    import concourse.bacc as bacc
    from concourse.bass_utils import run_bass_kernel_spmd

    a = {k: np.ascontiguousarray(v) for k, v in inputs.items()}

    def constant(shape):
        return np.zeros(shape, np.float32)

    def quads(rows):
        laid = np.zeros((QUAD, 32, 2, rows.shape[1]), np.float32)
        laid[:, 0:HD] = rows.reshape(2, QUAD, HD, -1).transpose(1, 2, 0, 3)
        return laid.reshape(128, 2, -1)

    cols = constant((128, len(COLS)))

    def put(name, v, rows=slice(0, 128)):
        cols[rows, COL[name]] = v

    put("norm_w", a["L0_conv_norm_w"])
    put("norm_b", a["L0_conv_norm_b"])
    for i, name in enumerate(("qb", "kb")):
        put(name, a["L0_conv_qkv_b"][i * C:(i + 1) * C])
    cols[:, [COL["vb0"], COL["vb1"]]] = quads(a["L0_conv_qkv_b"][2 * C:, None])[:, :, 0]
    put("pb", a["L0_conv_proj_b"])
    put("gn_w", a["L2_conv_gn_gamma"])
    put("gn_b", a["L2_conv_gn_beta"])
    for name in ("bq", "bk", "bv", "bo"):
        put(name, a["L2_conv_" + name])
    put("bcv", a["L1_conv_bcv"])
    put("b_so", a["L1_conv_b_so"])
    put("gamma", a["L1_conv_gamma"][0])
    put("beta", a["L1_conv_beta"][0])
    put("l3b", a["L3_conv_bias"])
    put("q1b", a["L1_conv_bq"], slice(0, IC))
    put("k1b", a["L1_conv_bk"], slice(0, IC))

    early = constant((128, E_WIDTH))
    channel = np.arange(128)
    early[:, E_AVG:E_AVG + 128] = (channel[:, None] // 4 == channel[None, :] // 4) * 0.25
    early[:, E_ID:E_ID + 128] = np.eye(128)
    early[:, E_ID32:E_ID32 + 32] = channel[:, None] % 32 == np.arange(32)[None, :]
    for pp in range(2):
        for hh in range(2):
            early[:, E_SHIFT + 2 * pp + hh] = (channel == 64 * pp + hh) | (channel == 64 * pp + hh + 2)
    early[:, E_COLS:] = cols

    sum_rows = (channel[:, None] == 32 * np.arange(QUAD)[None, :] + HD).astype(np.float32)
    inner = constant((C, 2, C))
    inner[:, 0, 0:IC], inner[:, 1, 0:IC] = a["L1_conv_wq"].T, a["L1_conv_wk"].T
    mid = np.concatenate([quads(a["L0_conv_proj_w"].T).reshape(128, 2 * C), inner.reshape(C, 2 * C),
                          a["L1_conv_wcq"].T, a["L1_conv_wck"].T, a["L1_conv_wcv"].T, sum_rows], 1)
    small = np.concatenate([a["L1_conv_wv"], a["L1_conv_w_so"].T, a["L1_conv_bv"][:, None]], 1)
    rows = np.concatenate([a["L1_conv_bcq"], a["L1_conv_bck"]])
    up, dn = a["L3_conv_up_filter"], a["L3_conv_down_filter"]
    up_rows = np.concatenate([np.repeat(toeplitz(up, 5 - 8 * nt, 8, -2, 4 * NEAR, 1), S, 0) for nt in range(NT)], 1)
    up_cols = np.tile(toeplitz(up, 5, S, -2, 32, 1), (8, 1))
    dn_rows = np.repeat(toeplitz(dn, 0, 4, -1, 8, 2), 32, 0)
    dn_cols = np.tile(toeplitz(dn, 6, 32, -1, S, 2), (4, 1))
    late = np.concatenate([a["L2_conv_wq"].T, a["L2_conv_wk"].T, a["L2_conv_wv"], a["L2_conv_wo"].T,
                           up_rows, up_cols, dn_rows, dn_cols], 1)
    arrays = {
        "x": a["x"].reshape(B, C, N), "early": early, "wqkv": np.ascontiguousarray(a["L0_conv_qkv_w"].T),
        "mid": np.ascontiguousarray(mid), "small": np.ascontiguousarray(small), "rows": rows,
        "late": np.ascontiguousarray(late),
    }
    nc = bacc.Bacc("TRN2", target_bir_lowering=False, num_devices=1)
    args = [nc.dram_tensor(f"in_{n}", v.shape, F32, kind="ExternalInput").ap() for n, v in arrays.items()]
    out = nc.dram_tensor("out", (B, C, N), F32, kind="ExternalOutput").ap()
    build(nc, *args, out)
    got = run_bass_kernel_spmd(nc, [{f"in_{n}": v for n, v in arrays.items()}], core_ids=[0])
    return got.results[0]["out"].reshape(B, C, S, S)
```

```python
from contextlib import ExitStack

import concourse.bass as bass
from concourse import mybir

F32 = mybir.dt.float32
F32R = mybir.dt.float32r
I32 = mybir.dt.int32
ALU = mybir.AluOpType
ACT = mybir.ActivationFunctionType
AX = mybir.AxisListType

C = 128
B = 2
S = 16
N = S * S
NT = N // 128
HEADS, HD = 8, 16
QUAD = 4
GROUPS = B * HEADS // QUAD
COMBOS = 4
IC = C // 8
TAPS = 12
BANDS = 8
NEAR = 6
PADTOP = 3
EPS0, EPS2 = 1e-5, 1e-6
WARM_STAT, WARM_NORM, WARM_NORM2 = 9, 7, (1, 0)
SLOPE, GAIN = 0.2, 2.0 ** 0.5
UP_GAIN = 4.0
SCALE0 = HD ** -0.5
SCALE2 = C ** -0.5
NORM_STEPS = 7
RSQRT_SEED, RSQRT_FIRST, RSQRT_GAIN = 1595932665.0 - 2.0 ** 30, 2.38924456, 0.703952253

COLS = "norm_w norm_b qb kb vb0 vb1 pb gn_w gn_b bq bk bv bo bcv b_so gamma beta l3b q1b k1b".split()
COL = {name: i for i, name in enumerate(COLS)}

E_AVG, E_ID, E_ID32, E_COLS = 0, 128, 256, 288
E_WIDTH = E_COLS + len(COLS)
A_PROJ, A_QK1, A_CQK, A_CV, A_SUM = 0, 256, 384, 640, 768
A_WIDTH = A_SUM + QUAD
L_Q, L_K, L_V, L_O, L_UR = 0, 128, 256, 384, 512
L_UC = L_UR + NT * 4 * NEAR
L_DR = L_UC + 32
L_DC = L_DR + 8
L_WIDTH = L_DC + S


def build(nc, x_in, early_in, wqkv_in, mid_in, small_in, rows_in, late_in, out):
    with ExitStack() as ctx:
        def sb(name, shape, dt=F32):
            return ctx.enter_context(nc.sbuf_tensor(name, shape, dt))

        def sem(name):
            return ctx.enter_context(nc.semaphore(name))

        bank = [ctx.enter_context(nc.psum_tensor(f"bank{i}", [128, 512], F32)) for i in range(8)]
        PASS1, PASS2, UBANK, TBANK = bank[0:2], bank[4:7], bank[2:4], bank[7]
        K0, K1, K2, K3 = (bank[0], bank[4]), (bank[1], bank[5]), (bank[3], bank[2]), (bank[7], bank[6])

        S1, P1 = (K0, K3), (K0, K3)
        S2, P2 = (K2, K0), (K1, K2)
        UP = ((K0[0], K1[0]), (K0[1], K1[1], K0[0], K1[0]))

        def part3(b, i):
            per = BANDS // len(UP[b])
            return slice(per * i, per * (i + 1)), b * len(UP[0]) + i + 1

        x = sb("x", [C, B, N])
        early = sb("early", [128, E_WIDTH])
        wqkv = sb("wqkv", [C, 3 * C])
        mid = sb("mid", [C, A_WIDTH])
        small = sb("small", [IC, 2 * C + 1])
        rows = sb("rows", [128, 2 * C])
        late = sb("late", [128, L_WIDTH])
        avg, ident = early[:, E_AVG:E_AVG + 128], early[:, E_ID:E_ID + 128]

        def col(name, end=128, start=0):
            i = E_COLS + COL[name]
            return early[start:end, i:i + 1]

        split_sel = sb("split_sel", [C, 4, 4, 128], F32R)
        identr = sb("identr", [128, 128], F32R)
        wfold = sb("wfold", [C, 2, C])
        derived = sb("derived", [C, 8])
        PB, B1, BCV, BQ2, B2, T0, T1 = (derived[:, i:i + 1] for i in range(7))
        upm = sb("upm", [128, NT, 4 * NEAR, 32])
        idle = sb("idle", [128, 128])
        warmed = sb("warmed", [128, 1])

        stat_raw = sb("stat_raw", [C, B, 6])
        stat = sb("stat", [C, B, 2])
        gn = sb("gn", [C, 8, B])
        hn = sb("hn", [C, B, N])
        q_hi, q_lo = sb("q_hi", [C, B, N], F32R), sb("q_lo", [C, B, N], F32R)
        k_hi, k_lo = sb("k_hi", [C, B, N], F32R), sb("k_lo", [C, B, N], F32R)
        qs, ks = sb("qs", [128, 4, 2, B, N], F32R), sb("ks", [128, 4, 2, B, N], F32R)
        vt = sb("vt", [128, B, NT, HEADS, 32])
        negmax = sb("negmax", [128, 2, NT, 2, 2])
        nm = sb("nm", [128, 2, NT, 2, 2, 32], F32R)
        p0 = sb("p0", [128, 2, NT, 2, 2, N])
        us = sb("us", [128, B, 2, N])
        rsum = sb("rsum", [128, 2, NT, QUAD])
        rwide = sb("rwide", [128, 2, NT, QUAD, 32])
        un = sb("un", [128, B, 2, N])
        xb = sb("xb", [C, B, N])
        x1 = sb("x1", [C, B, N])
        qk1 = sb("qk1", [64, B, 2, N])
        cqk = sb("cqk", [128, B, NT, 2 * C])
        v1t = sb("v1t", [128, B, NT, C])
        vc = sb("vc", [C, B, N])
        red1 = sb("red1", [128, B, 3, NT + 1])
        p1 = sb("p1", [128, B, NT, N])
        p1n = sb("p1n", [128, B, NT, N])
        p1t = sb("p1t", [128, B, NT, N])
        pc = sb("pc", [128, B, 2, C])
        pct = sb("pct", [128, B, C])
        x1b = sb("x1b", [C, B, N])
        x2 = sb("x2", [C, B, N])
        stat_raw2 = sb("stat_raw2", [C, B, 6])
        stat2 = sb("stat2", [C, B, 2])
        gn2 = sb("gn2", [C, B, 8])
        hn2 = sb("hn2", [C, B, N])
        q2, k2 = sb("q2", [C, B, N]), sb("k2", [C, B, N])
        vx = sb("vx", [128, B, 2, NT, C])
        red2 = sb("red2", [128, B, 3, NT])
        p2 = sb("p2", [128, B, NT, N])
        p2t = sb("p2t", [128, B, NT, N])
        x2b = sb("x2b", [C, B, N])
        x3t = sb("x3t", [128, B, NT, C])
        sloped = sb("sloped", [128, B, BANDS, C])
        z = sb("z", [128, B, BANDS, C])
        down = sb("down", [128, 128])
        y = sb("y", [C, B, N])

        s = {name: sem(name) for name in (
            "x_in early_in wqkv_in mid_in small_in rows_in late_in out_done "
            "idle_made sel_zero sel_made qs_zero ks_ones_top ks_ones_bottom identr_made nm_zero vt_ones "
            "xb_made x1b_made x2b_made fold_made fold_saved derived_made "
            "dve_chain stat_made gavg_made stat_step norm_made norm_step hn_made q_made k_made v_made "
            "q_hi_made k_hi_made q_lo_made k_lo_made vt_made q_tile_made k_tile_made "
            "q_saved_top q_saved_bottom_act q_saved_bottom_dve k_saved_top k_saved_bottom "
            "pass1_made max_made nm_made nmt_made nmt_saved pass2_made exp_made pv_made "
            "us_saved sums_made inverse_made spread_made un_made proj_made x1_made "
            "qk1_made q1_saved k1_saved cqk_made cqk_saved v1_made v1_saved "
            "s1_made max1_made exp1_made inverse1_made p1n_made p1t_made p1t_saved_act p1t_saved_dve "
            "e_made maxe_made expe_made pc_made pct_made pct_saved o1_made x2_made "
            "hn2_made q2_made k2_made v2_made x2t_made q2_saved k2_saved v2_saved "
            "s2_made max2_made exp2_made p2t_made p2t_saved_act p2t_saved_dve o2_made x3_made "
            "up_made sloped_made z_made upm_made down_saved y_made y_saved").split()}

        block = ctx.enter_context(nc.Block())

        @block.sync
        def _(sp):
            sp.dma_start(x[:, :, :], x_in.rearrange("b c n -> c b n")).then_inc(s["x_in"], 16)
            sp.dma_start(wqkv[:, :], wqkv_in).then_inc(s["wqkv_in"], 16)
            sp.dma_start(small[:, :], small_in).then_inc(s["small_in"], 16)
            sp.dma_start(late[:, :], late_in).then_inc(s["late_in"], 16)
            for b in range(B):
                sp.wait_ge(s["y_saved"], b + 1)
                sp.dma_start(out[b], y[:, b, :]).then_inc(s["out_done"], 16)
            sp.wait_ge(s["out_done"], 16 * B)

        @block.gpsimd
        def _(pool):
            pool.memset(split_sel[:, :, :, :].bitcast(F32), 0.0).then_inc(s["sel_zero"], 1)
            pool.memset(nm[:, :, :, :, :, :].bitcast(F32), 0.0).then_inc(s["nm_zero"], 1)
            pool.wait_ge(s["sel_zero"], 1)
            pool.wait_ge(s["nm_zero"], 1)
            pool.memset(ks[64:128, :, 0, :, :].bitcast(F32), 1.0).then_inc(s["ks_ones_bottom"], 1)
            pool.wait_ge(s["ks_ones_bottom"], 1)
            pool.wait_ge(s["early_in"], 16)
            for p in range(4):
                block32 = early[32 * p:32 * p + 32, E_ID32:E_ID32 + 32].rearrange("p (h d) -> p h d", h=2)
                src = block32.unsqueeze(2).broadcast_to([32, 2, 2, HD])
                for kind, first, step in ((0, 0, 1), (1, 2, 1), (2, 0, 2), (3, 1, 2)):
                    dst = split_sel[32 * p:32 * p + 32, kind, p, :].rearrange(
                        "p (h r d) -> p h r d", h=2, r=COMBOS)[:, :, first:first + step + 1:step, :]
                    pool.tensor_copy(dst, src).then_inc(s["sel_made"], 1)
                pool.wait_ge(s["sel_made"], 4 * p + 4)
            pool.tensor_copy(identr[:, :], ident).then_inc(s["identr_made"], 1)
            pool.wait_ge(s["identr_made"], 1)
            for hh in range(2):
                other = slice(64 * (1 - hh), 64 * (1 - hh) + 64)
                pool.memset(qs[other, :, hh, :, :].bitcast(F32), 0.0).then_inc(s["qs_zero"], 1)
                pool.wait_ge(s["qs_zero"], hh + 1)
            pool.memset(vt[:, :, :, :, HD:32], 1.0).then_inc(s["vt_ones"], 1)
            pool.wait_ge(s["x_in"], 16)
            pool.wait_ge(s["derived_made"], 1)
            pool.tensor_scalar(xb[:, :, :], x[:, :, :], PB, None, ALU.add).then_inc(s["xb_made"], 1)
            pool.wait_ge(s["late_in"], 16)
            for nt in range(NT):
                taps = late[:, L_UR + nt * 4 * NEAR:L_UR + (nt + 1) * 4 * NEAR]
                pool.tensor_tensor(upm[:, nt, :, :], taps.unsqueeze(2).broadcast_to([128, 4 * NEAR, 32]),
                                   late[:, L_UC:L_UC + 32].unsqueeze(1).broadcast_to([128, 4 * NEAR, 32]),
                                   ALU.mult).then_inc(s["upm_made"], 1)
            for b in range(B):
                pool.wait_ge(s["x1_made"], b + 1)
                pool.tensor_scalar(x1b[:, b, :], x1[:, b, :], 2.0, B1, ALU.mult, ALU.add).then_inc(s["x1b_made"], 1)
            for b in range(B):
                pool.wait_ge(s["x2_made"], b + 1)
                pool.tensor_scalar(x2b[:, b, :], x2[:, b, :], B2, None, ALU.add).then_inc(s["x2b_made"], 1)

        @block.tensor
        def _(pe):
            def mm(o, lhsT, rhs, start=True, stop=True):
                return pe.matmul(o, lhsT, rhs, start=start, stop=stop, skip_group_check=True)

            def warm(n, o=bank[3]):
                for _ in range(n):
                    mm(o[:, 0:128], idle[:, :], idle[:, :])

            def project0():
                pe.wait_ge(s["idle_made"], 1)
                warm(WARM_STAT)
                pe.wait_ge(s["early_in"], 16)
                pe.wait_ge(s["stat_made"], 1)
                mm(TBANK[:, 0:2 * B], avg, stat[:, :, :].rearrange("p b c -> p (b c)")).then_inc(s["gavg_made"], 1)
                warm(WARM_NORM)
                pe.wait_ge(s["wqkv_in"], 16)
                pe.wait_ge(s["hn_made"], B)
                flat = hn[:, :, :].rearrange("p b n -> p (b n)")
                mm(bank[0][:, :], wqkv[:, 0:C], flat).then_inc(s["q_made"], 1)
                mm(bank[1][:, :], wqkv[:, C:2 * C], flat).then_inc(s["k_made"], 1)
                for t in range(B * NT):
                    last = mm(bank[2][:, t * C:(t + 1) * C], flat[:, t * 128:(t + 1) * 128], wqkv[:, 2 * C:3 * C])
                last.then_inc(s["v_made"], 1)

            def fold():
                pe.wait_ge(s["mid_in"], 16)
                pe.wait_ge(s["small_in"], 16)
                pe.wait_ge(s["late_in"], 16)
                mm(bank[3][:, 0:C], small[:, 0:C], small[:, C:2 * C])
                mm(bank[3][:, C:2 * C], late[:, L_V:L_V + C], late[:, L_O:L_O + C])
                for g in range(2):
                    mm(bank[3][:, 256:257], mid[:, A_PROJ + g * C:A_PROJ + (g + 1) * C], col(f"vb{g}"), g == 0, g == 1)
                mm(bank[3][:, 257:258], small[:, C:2 * C], small[:, 2 * C:2 * C + 1])
                mm(bank[3][:, 258:259], late[:, L_O:L_O + C], col("bv")).then_inc(s["fold_made"], 1)

            def wait_k(p):
                pe.wait_ge(s["k_saved_top"], p + 1)
                pe.wait_ge(s["k_saved_bottom"], p + 1)

            def wait_q(p):
                pe.wait_ge(s["q_saved_top"], p + 1)
                pe.wait_ge(s["q_saved_bottom_dve"], min(p + 1, 2))
                if p > 1:
                    pe.wait_ge(s["q_saved_bottom_act"], p - 1)

            def tile(i):
                p, kind = i // 2, 2 * (i % 2)
                hi, lo = (q_hi, q_lo) if kind == 0 else (k_hi, k_lo)
                if i == 0:
                    pe.wait_ge(s["sel_made"], 16)
                if i < 2:
                    pe.wait_ge(s["k_hi_made" if kind else "q_hi_made"], 1)
                if i >= 4:
                    if i % 2:
                        wait_k(p - 2)
                    else:
                        wait_q(p - 2)
                o = bank[4 + i % 4]
                mm(o[:, :], split_sel[:, kind, p, :], hi[:, :, :].rearrange("p b n -> p (b n)"), True, False)
                if i < 2:
                    pe.wait_ge(s["k_lo_made" if kind else "q_lo_made"], 1)
                mm(o[:, :], split_sel[:, kind + 1, p, :], lo[:, :, :].rearrange("p b n -> p (b n)"),
                   False, True).then_inc(s["k_tile_made" if i % 2 else "q_tile_made"], 1)

            def pass1(G, u):
                b, g, nt, pp, n = G // 2, G % 2, u // 2, u % 2, 4 * G + u
                if n == 0:
                    pe.wait_ge(s["qs_zero"], 2)
                    pe.wait_ge(s["ks_ones_top"], 1)
                    pe.wait_ge(s["ks_ones_bottom"], 1)
                if G < 2 and nt == 0:
                    wait_q(2 * g + pp)
                    wait_k(2 * g + pp)
                if n >= 2:
                    pe.wait_ge(s["max_made"], n - 1)
                for hh in range(2):
                    other = 1 - hh
                    last = mm(PASS1[pp][:, other * N:(other + 1) * N],
                              qs[:, 2 * g + pp, hh, b, nt * 128:(nt + 1) * 128], ks[:, 2 * g + pp, hh, b, :])
                last.then_inc(s["pass1_made"], 1)

            def shift_rows(G):
                if G == 0:
                    pe.wait_ge(s["identr_made"], 1)
                    wait_k(3)
                pe.wait_ge(s["nm_made"], G + 1)
                if G >= 1:
                    pe.wait_ge(s["nmt_saved"], 4 * G)
                for nt in range(NT):
                    last = mm(TBANK[:, nt * 128:(nt + 1) * 128],
                              nm[:, G % 2, nt, :, :, :].rearrange("p o q c -> p (o q c)"), identr[:, :])
                last.then_inc(s["nmt_made"], 1)

            def pass2(G, v):
                b, g, mt, pp, n = G // 2, G % 2, v // 2, v % 2, 4 * G + v
                if n >= 3:
                    pe.wait_ge(s["exp_made"], n - 2)
                pe.wait_ge(s["nmt_saved"], 4 * G + 2 * pp + 2)
                for hh in range(2):
                    last = mm(PASS2[n % 3][:, hh * N:(hh + 1) * N], ks[:, 2 * g + pp, hh, b, mt * 128:(mt + 1) * 128],
                              qs[:, 2 * g + pp, hh, b, :])
                last.then_inc(s["pass2_made"], 1)

            def values(G, mt):
                b, g = G // 2, G % 2
                if G == 0 and mt == 0:
                    pe.wait_ge(s["vt_ones"], 1)
                    pe.wait_ge(s["vt_made"], 1)
                if G == 1 and mt == 0:
                    pe.wait_ge(s["fold_saved"], 1)
                    pe.wait_ge(s["derived_made"], 1)
                if G == 2 and mt == 0:
                    pe.wait_ge(s["un_made"], 1)
                if G == 3 and mt == 0:
                    pe.wait_ge(s["x1_made"], 1)
                pe.wait_ge(s["exp_made"], 4 * G + 2 * mt + 2)
                for j in range(QUAD):
                    last = mm(UBANK[g][32 * j:32 * j + 32, 0:N], vt[:, b, mt, 4 * g + j, :],
                              p0[:, G % 2, mt, j // 2, j % 2, :], mt == 0, mt == NT - 1)
                last.then_inc(s["pv_made"], 1)

            def sums(G):
                b, g = G // 2, G % 2
                pe.wait_ge(s["us_saved"], G + 1)
                for nt in range(NT):
                    last = mm(UBANK[g][:, N + nt * QUAD:N + (nt + 1) * QUAD], us[:, b, g, nt * 128:(nt + 1) * 128],
                              mid[:, A_SUM:A_SUM + QUAD])
                last.then_inc(s["sums_made"], 1)

            def spread(G):
                g = G % 2
                pe.wait_ge(s["inverse_made"], G + 1)
                for nt in range(NT):
                    last = pe.transpose(UBANK[g][:, N + nt * 128:N + (nt + 1) * 128],
                                        rwide[:, g, nt, :, :].rearrange("p j d -> p (j d)"), ident)
                last.then_inc(s["spread_made"], 1)

            def project_out(b, g):
                pe.wait_ge(s["un_made"], 3 if (b, g) == (1, 0) else 2 * b + 2)
                last = mm(UBANK[1 - b][:, 0:N], mid[:, A_PROJ + g * C:A_PROJ + (g + 1) * C], un[:, b, g, :],
                          g == 0, g == 1)
                if g == 1:
                    last.then_inc(s["proj_made"], 1)

            def queries1(b):
                if b == 0:
                    pe.wait_ge(s["max_made"], 4 * GROUPS)
                    pe.wait_ge(s["nmt_saved"], 4 * GROUPS)
                else:
                    pe.wait_ge(s["exp_made"], 4 * GROUPS)
                pe.wait_ge(s["x1_made"], b + 1)
                mm(K0[b][:, 0:N], mid[:, A_QK1:A_QK1 + C], x1[:, b, :]).then_inc(s["qk1_made"], 1)

            def channels1(b):
                for nt in range(NT):
                    last = mm(K1[b][:, nt * N:(nt + 1) * N], x1[:, b, nt * 128:(nt + 1) * 128],
                              mid[:, A_CQK:A_CQK + 2 * C])
                last.then_inc(s["cqk_made"], 1)

            def values1(b):
                pe.wait_ge(s["fold_saved"], 1)
                if b == 0:
                    pe.wait_ge(s["us_saved"], GROUPS)
                    pe.wait_ge(s["un_made"], GROUPS)
                for nt in range(NT):
                    mm(K2[b][:, nt * 128:(nt + 1) * 128], x1[:, b, nt * 128:(nt + 1) * 128], wfold[:, 0, :])
                mm(K2[b][:, N:2 * N], mid[:, A_CV:A_CV + C], x1[:, b, :]).then_inc(s["v1_made"], 1)

            def scores1(b):
                pe.wait_ge(s["q1_saved"], b + 1)
                pe.wait_ge(s["k1_saved"], b + 1)
                for nt in range(NT):
                    mm(S1[nt][b][:, 0:N], qk1[:, b, 0, nt * 128:(nt + 1) * 128],
                       qk1[:, b, 1, :]).then_inc(s["s1_made"], 1)

            def channel_scores1(b):
                pe.wait_ge(s["cqk_saved"], b + 1)
                for nt in range(NT):
                    last = mm(K1[b][:, 0:C], cqk[:, b, nt, 0:C], cqk[:, b, nt, C:2 * C], nt == 0, nt == NT - 1)
                last.then_inc(s["e_made"], 1)

            def turn_p1(b, nt):
                pe.wait_ge(s["p1n_made"], NT * b + nt + 1)
                for mt in range(NT):
                    last = pe.transpose(P1[nt][b][:, mt * 128:(mt + 1) * 128],
                                        p1n[:, b, nt, mt * 128:(mt + 1) * 128], ident)
                last.then_inc(s["p1t_made"], 1)

            def turn_pc(b):
                pe.wait_ge(s["pc_made"], b + 1)
                pe.transpose(K1[b][:, 0:C], pc[:, b, 1, :], ident).then_inc(s["pct_made"], 1)

            def output1(b):
                pe.wait_ge(s["v1_saved"], b + 1)
                pe.wait_ge(s["pct_saved"], b + 1)
                mm(K2[b][:, 0:N], pct[:, b, :], vc[:, b, :], True, False)
                pe.wait_ge(s["p1t_saved_dve"], b + 1)
                pe.wait_ge(s["p1t_saved_act"], b + 1)
                for mt in range(NT):
                    last = mm(K2[b][:, 0:N], v1t[:, b, mt, :], p1t[:, b, mt, :], False, mt == NT - 1)
                last.then_inc(s["o1_made"], 1)

            def average2(b):
                pe.wait_ge(s["stat_made"], b + 2)
                mm(K2[b][:, 0:2], avg, stat2[:, b, :]).then_inc(s["gavg_made"], 1)

            def project2(b):
                warm(WARM_NORM2[b], K0[b])
                pe.wait_ge(s["hn2_made"], b + 1)
                mm(K0[b][:, 0:N], late[:, L_Q:L_Q + C], hn2[:, b, :]).then_inc(s["q2_made"], 1)
                mm(K1[b][:, 0:N], late[:, L_K:L_K + C], hn2[:, b, :]).then_inc(s["k2_made"], 1)

            def values2(b):
                for nt in range(NT):
                    last = mm(K3[b][:, nt * 128:(nt + 1) * 128], hn2[:, b, nt * 128:(nt + 1) * 128], wfold[:, 1, :])
                last.then_inc(s["v2_made"], 1)

            def turn_x2(b):
                pe.wait_ge(s["x2b_made"], b + 1)
                for nt in range(NT):
                    last = pe.transpose(K3[b][:, (NT + nt) * 128:(NT + nt + 1) * 128],
                                        x2b[:, b, nt * 128:(nt + 1) * 128], ident)
                last.then_inc(s["x2t_made"], 1)

            def scores2(b):
                pe.wait_ge(s["q2_saved"], b + 1)
                pe.wait_ge(s["k2_saved"], b + 1)
                for nt in range(NT):
                    mm(S2[nt][b][:, 0:N], q2[:, b, nt * 128:(nt + 1) * 128], k2[:, b, :]).then_inc(s["s2_made"], 1)

            def turn_p2(b, nt):
                pe.wait_ge(s["exp2_made"], NT * b + nt + 1)
                for mt in range(NT):
                    last = pe.transpose(P2[nt][b][:, mt * 128:(mt + 1) * 128],
                                        p2[:, b, nt, mt * 128:(mt + 1) * 128], ident)
                last.then_inc(s["p2t_made"], 1)

            def output2(b):
                pe.wait_ge(s["v2_saved"], b + 1)
                for nt in range(NT):
                    pe.wait_ge(s[("p2t_saved_act", "p2t_saved_dve")[nt]], b + 1)
                    for mt in range(NT):
                        last = mm(K3[b][:, nt * C:(nt + 1) * C], p2t[:, b, nt, mt * 128:(mt + 1) * 128],
                                  vx[:, b, 0, mt, :], mt == 0, mt == NT - 1)
                last.then_inc(s["o2_made"], 1)

            def up3(b, i):
                bands, _ = part3(b, i)
                if i == 0:
                    pe.wait_ge(s["upm_made"], NT)
                if i == 2:
                    pe.wait_ge(s["z_made"], len(UP[0]))
                for t in range(bands.start, bands.stop):
                    tiles = [nt for nt in range(NT) if 0 <= t - 2 * nt < NEAR]
                    for nt in tiles:
                        if t == 2 * nt:
                            pe.wait_ge(s["x3_made"], NT * b + nt + 1)
                        last = mm(UP[b][i][:, (t - bands.start) * C:(t - bands.start + 1) * C],
                                  upm[:, nt, 4 * (t - 2 * nt):4 * (t - 2 * nt) + 4, :].rearrange("p y x -> p (y x)"),
                                  x3t[:, b, nt, :], nt == tiles[0], nt == tiles[-1])
                last.then_inc(s["up_made"], 1)

            def down3(b, i):
                bands, count = part3(b, i)
                if i == 0:
                    pe.wait_ge(s["down_saved"], 1)
                pe.wait_ge(s["z_made"], count)
                for t in range(bands.start, bands.stop):
                    last = mm(K2[b][:, 32 * t:32 * t + 128], z[:, b, t, :], down[:, :], t == 0, t == BANDS - 1)
                if bands.stop == BANDS:
                    last.then_inc(s["y_made"], 1)

            project0()
            tile(0)
            tile(1)
            tile(2)
            tile(3)
            pass1(0, 0)
            tile(4)
            pass1(0, 1)
            tile(5)
            tile(6)
            pass1(0, 2)
            pass1(0, 3)
            tile(7)
            fold()
            pass1(1, 0)
            wait_k(3)
            pass1(1, 1)
            shift_rows(0)
            wait_q(3)
            pass1(1, 2)
            pass2(0, 0)
            pass1(1, 3)
            pass2(0, 1)
            pass2(0, 2)
            pass2(0, 3)
            for G in range(1, GROUPS - 1):
                pass1(G + 1, 0)
                pass1(G + 1, 1)
                shift_rows(G)
                values(G - 1, 0)
                values(G - 1, 1)
                pass1(G + 1, 2)
                pass2(G, 0)
                pass1(G + 1, 3)
                pass2(G, 1)
                sums(G - 1)
                pass2(G, 2)
                pass2(G, 3)
                spread(G - 1)
            values(2, 0)
            shift_rows(3)
            values(2, 1)
            project_out(0, 0)
            pass2(3, 0)
            project_out(0, 1)
            pass2(3, 1)
            sums(2)
            pass2(3, 2)
            pass2(3, 3)
            queries1(0)
            spread(2)
            values(3, 0)
            values(3, 1)
            channels1(0)
            sums(3)
            scores1(0)
            spread(3)
            project_out(1, 0)
            channel_scores1(0)
            project_out(1, 1)
            values1(0)
            queries1(1)
            channels1(1)
            turn_p1(0, 0)
            turn_p1(0, 1)
            turn_pc(0)
            scores1(1)
            output1(0)
            values1(1)
            average2(0)
            channel_scores1(1)
            turn_p1(1, 0)
            turn_x2(0)
            project2(0)
            turn_pc(1)
            turn_p1(1, 1)
            output1(1)
            scores2(0)
            average2(1)
            turn_x2(1)
            turn_p2(0, 0)
            turn_p2(0, 1)
            values2(0)
            project2(1)
            output2(0)
            scores2(1)
            up3(0, 0)
            up3(0, 1)
            turn_p2(1, 0)
            values2(1)
            turn_p2(1, 1)
            down3(0, 0)
            output2(1)
            down3(0, 1)
            up3(1, 0)
            up3(1, 1)
            up3(1, 2)
            up3(1, 3)
            down3(1, 0)
            down3(1, 1)
            down3(1, 2)
            down3(1, 3)

        @block.scalar
        def _(act):
            act.dma_start(early[:, :], early_in).then_inc(s["early_in"], 16)
            act.dma_start(mid[:, :], mid_in).then_inc(s["mid_in"], 16)
            act.dma_start(rows[:, :], rows_in.partition_broadcast(128)).then_inc(s["rows_in"], 16)

            act.wait_ge(s["idle_made"], 1)
            act.activation(warmed[:, :], idle[:, 0:1], ACT.Exp)

            def norm0():
                act.wait_ge(s["x_in"], 16)
                act.wait_ge(s["early_in"], 16)
                act.wait_ge(s["norm_made"], 1)
                act.activation(hn[:, 1, :], x[:, 1, :], ACT.Identity, bias=gn[:, 7, 1:2],
                               scale=gn[:, 6, 1:2]).then_inc(s["hn_made"], 1)

            def high_q():
                act.wait_ge(s["q_made"], 1)
                act.activation(q_hi[:, :, :].rearrange("p b n -> p (b n)"), bank[0][:, :], ACT.Identity,
                               bias=col("qb")).then_inc(s["q_hi_made"], 1)

            def high_k():
                act.wait_ge(s["k_made"], 1)
                act.activation(k_hi[:, :, :].rearrange("p b n -> p (b n)"), bank[1][:, :], ACT.Identity,
                               bias=col("kb")).then_inc(s["k_hi_made"], 1)

            def save_vt():
                act.wait_ge(s["v_made"], 1)
                act.activation(vt[:, :, :, :, 0:HD].rearrange("p b t h d -> p (b t h) d"),
                               bank[2][:, :].rearrange("p (h d) -> p h d", d=HD), ACT.Copy).then_inc(s["vt_made"], 1)

            def save_q_top(p):
                act.wait_ge(s["q_tile_made"], p + 1)
                act.activation(qs[0:64, p, 0, :, :].rearrange("p b n -> p (b n)"), bank[4 + 2 * p % 4][0:64, :],
                               ACT.Copy).then_inc(s["q_saved_top"], 1)

            def save_q_bottom(p):
                act.wait_ge(s["q_tile_made"], p + 1)
                act.activation(qs[64:128, p, 1, :, :].rearrange("p b n -> p (b n)"), bank[4 + 2 * p % 4][64:128, :],
                               ACT.Copy).then_inc(s["q_saved_bottom_act"], 1)

            def save_k_top(p):
                act.wait_ge(s["k_tile_made"], p + 1)
                act.activation(ks[0:64, p, 0, :, :].rearrange("p b n -> p (b n)"), bank[5 + 2 * p % 4][0:64, :],
                               ACT.Copy).then_inc(s["k_saved_top"], 1)

            def save_fold():
                act.wait_ge(s["fold_made"], 1)
                act.activation(wfold[:, :, :].rearrange("p k c -> p (k c)"), bank[3][:, 0:2 * C],
                               ACT.Copy).then_inc(s["fold_saved"], 1)

            def save_shift(G, pp):
                act.wait_ge(s["nmt_made"], G + 1)
                for hh in range(2):
                    first = 64 * (1 - hh) + 32 * pp
                    act.activation(qs[first:first + 32, 2 * (G % 2) + pp, hh, G // 2, :],
                                   TBANK[first:first + 32, 0:N], ACT.Copy).then_inc(s["nmt_saved"], 1)

            def exp0(G, v):
                act.wait_ge(s["pass2_made"], 4 * G + v + 1)
                if G >= 2:
                    act.wait_ge(s["pv_made"], 2 * (G - 2) + v // 2 + 1)
                act.activation(p0[:, G % 2, v // 2, v % 2, :, :].rearrange("p a n -> p (a n)"),
                               PASS2[(4 * G + v) % 3][:, :], ACT.Exp, scale=SCALE0).then_inc(s["exp_made"], 1)

            def save_u(G):
                act.wait_ge(s["pv_made"], 2 * G + 2)
                act.activation(us[:, G // 2, G % 2, :], UBANK[G % 2][:, 0:N], ACT.Copy).then_inc(s["us_saved"], 1)

            def save_q1(b):
                act.wait_ge(s["qk1_made"], b + 1)
                act.activation(qk1[:, b, 0, :], K0[b][0:64, 0:N], ACT.Identity,
                               bias=col("q1b", 64)).then_inc(s["q1_saved"], 1)

            def save_v1(b):
                act.wait_ge(s["v1_made"], b + 1)
                act.wait_ge(s["derived_made"], 1)
                act.activation(v1t[:, b, :, :].rearrange("p t c -> p (t c)"), K2[b][:, 0:N], ACT.Copy)
                act.activation(vc[:, b, :], K2[b][:, N:2 * N], ACT.Identity, bias=BCV,
                               scale=col("beta")).then_inc(s["v1_saved"], 1)

            def exp1(b, nt):
                act.wait_ge(s["max1_made"], NT * b + nt + 1)
                act.activation(p1[:, b, nt, :], S1[nt][b][:, 0:N], ACT.Exp, bias=red1[:, b, 0, nt:nt + 1],
                               accum_out=red1[:, b, 1, nt:nt + 1]).then_inc(s["exp1_made"], 1)

            def exp_channels1(b):
                act.wait_ge(s["maxe_made"], b + 1)
                act.activation(pc[:, b, 0, :], K1[b][:, 0:C], ACT.Exp, bias=red1[:, b, 0, NT:NT + 1],
                               accum_out=red1[:, b, 1, NT:NT + 1]).then_inc(s["expe_made"], 1)

            def save_pct(b):
                act.wait_ge(s["pct_made"], b + 1)
                act.activation(pct[:, b, :], K1[b][:, 0:C], ACT.Copy).then_inc(s["pct_saved"], 1)

            def save_p1t(b):
                act.wait_ge(s["p1t_made"], NT * b + 1)
                act.activation(p1t[:, b, :, 0:128], P1[0][b][:, 0:N].rearrange("p (t n) -> p t n", t=NT),
                               ACT.Copy).then_inc(s["p1t_saved_act"], 1)

            def save_q2(b):
                act.wait_ge(s["q2_made"], b + 1)
                act.activation(q2[:, b, :], K0[b][:, 0:N], ACT.Identity, bias=BQ2,
                               scale=SCALE2).then_inc(s["q2_saved"], 1)

            def save_v2(b):
                act.wait_ge(s["v2_made"], b + 1)
                act.wait_ge(s["x2t_made"], b + 1)
                act.activation(vx[:, b, :, :, :].rearrange("p k t c -> p (k t c)"), K3[b][:, :],
                               ACT.Copy).then_inc(s["v2_saved"], 1)

            def exp2(b, nt):
                act.wait_ge(s["max2_made"], NT * b + nt + 1)
                act.activation(p2[:, b, nt, :], S2[nt][b][:, 0:N], ACT.Exp, bias=red2[:, b, 0, nt:nt + 1],
                               accum_out=red2[:, b, 1, nt:nt + 1]).then_inc(s["exp2_made"], 1)

            def save_p2t(b):
                act.wait_ge(s["p2t_made"], NT * b + 1)
                act.activation(p2t[:, b, 0, :], P2[0][b][:, 0:N], ACT.Copy).then_inc(s["p2t_saved_act"], 1)

            def slope3(b, i):
                bands, count = part3(b, i)
                act.wait_ge(s["up_made"], count)
                act.activation(sloped[:, b, bands, :].rearrange("p t c -> p (t c)"),
                               UP[b][i][:, 0:(bands.stop - bands.start) * C], ACT.Copy,
                               scale=SLOPE).then_inc(s["sloped_made"], 1)

            norm0()
            high_q()
            high_k()
            save_q_top(0)
            save_k_top(0)
            save_q_top(1)
            save_k_top(1)
            save_q_bottom(2)
            save_q_top(2)
            save_q_top(3)
            save_q_bottom(3)
            save_k_top(2)
            save_k_top(3)
            save_fold()
            save_vt()
            save_shift(0, 0)
            save_shift(0, 1)
            exp0(0, 0)
            exp0(0, 1)
            exp0(0, 2)
            exp0(0, 3)
            for G in range(1, GROUPS - 1):
                save_shift(G, 0)
                save_shift(G, 1)
                save_u(G - 1)
                exp0(G, 0)
                exp0(G, 1)
                exp0(G, 2)
                exp0(G, 3)
            save_shift(3, 0)
            save_shift(3, 1)
            save_u(2)
            exp0(3, 0)
            exp0(3, 1)
            exp0(3, 2)
            exp0(3, 3)
            save_u(3)
            save_q1(0)
            exp1(0, 0)
            exp1(0, 1)
            exp_channels1(0)
            save_v1(0)
            save_q1(1)
            save_pct(0)
            save_p1t(0)
            exp1(1, 0)
            exp1(1, 1)
            exp_channels1(1)
            save_v1(1)
            save_p1t(1)
            save_q2(0)
            save_pct(1)
            exp2(0, 0)
            exp2(0, 1)
            save_p2t(0)
            save_v2(0)
            save_q2(1)
            exp2(1, 0)
            slope3(0, 0)
            exp2(1, 1)
            slope3(0, 1)
            save_p2t(1)
            save_v2(1)
            slope3(1, 0)
            slope3(1, 1)
            slope3(1, 2)
            slope3(1, 3)

        @block.vector
        def _(dve):
            done = [0]

            def then(instruction):
                done[0] += 1
                instruction.then_inc(s["dve_chain"], 1)
                dve.wait_ge(s["dve_chain"], done[0])

            def group_norm(step, averages, w, bias, temps):
                for g, t in zip(averages, temps):
                    if step == 0:
                        last = dve.tensor_scalar(t[0], g[:, 0:1], g[:, 0:1], g[:, 1:2], ALU.mult, ALU.subtract)
                    elif step == 1:
                        last = dve.tensor_scalar(t[1].bitcast(I32), t[0].bitcast(I32), -0.5, RSQRT_SEED,
                                                 ALU.mult, ALU.add)
                    elif step == 2:
                        dve.tensor_scalar(t[2], t[0], 0.5 * RSQRT_GAIN ** 2, None, ALU.mult)
                        last = dve.scalar_tensor_tensor(out=t[3], in0=t[1], scalar=t[1], in1=t[0],
                                                        op0=ALU.mult, op1=ALU.mult)
                    elif step == 3:
                        last = dve.scalar_tensor_tensor(out=t[4], in0=t[3], scalar=RSQRT_FIRST, in1=t[1],
                                                        op0=ALU.add, op1=ALU.mult)
                    elif step == 4:
                        dve.scalar_tensor_tensor(out=t[5], in0=t[4], scalar=t[4], in1=t[2], op0=ALU.mult, op1=ALU.mult)
                        dve.tensor_scalar(t[3], t[4], w, RSQRT_GAIN, ALU.mult, ALU.mult)
                        last = dve.tensor_scalar(t[1], t[4], w, -RSQRT_GAIN, ALU.mult, ALU.mult)
                    elif step == 5:
                        dve.scalar_tensor_tensor(out=t[6], in0=t[5], scalar=1.5, in1=t[3], op0=ALU.add, op1=ALU.mult)
                        last = dve.scalar_tensor_tensor(out=t[0], in0=t[5], scalar=1.5, in1=t[1],
                                                        op0=ALU.add, op1=ALU.mult)
                    else:
                        last = dve.scalar_tensor_tensor(out=t[7], in0=g[:, 0:1], scalar=t[0], in1=bias,
                                                        op0=ALU.mult, op1=ALU.add)
                return last

            def norm0():
                dve.memset(idle[:, :], 0.0).then_inc(s["idle_made"], 1)
                dve.memset(ks[0:64, :, 1, :, :].bitcast(F32), 1.0).then_inc(s["ks_ones_top"], 1)
                dve.wait_ge(s["x_in"], 16)
                for b in range(B):
                    last = dve.bn_stats(stat_raw[:, b, :], x[:, b, :])
                then(last)
                for b in range(B):
                    last = dve.bn_aggr(stat[:, b, :], stat_raw[:, b, :])
                then(last)
                then(dve.tensor_tensor(gn[:, 0, :], stat[:, :, 0], stat[:, :, 0], ALU.mult))
                dve.scalar_tensor_tensor(out=stat[:, :, 1], in0=gn[:, 0, :], scalar=EPS0, in1=stat[:, :, 1],
                                         op0=ALU.add, op1=ALU.add).then_inc(s["stat_made"], 1)
                dve.wait_ge(s["early_in"], 16)
                dve.wait_ge(s["gavg_made"], 1)
                averages = [TBANK[:, 2 * b:2 * b + 2] for b in range(B)]
                temps = [[gn[:, i, b:b + 1] for i in range(8)] for b in range(B)]
                for step in range(NORM_STEPS):
                    last = group_norm(step, averages, col("norm_w"), col("norm_b"), temps)
                    if step + 1 < NORM_STEPS:
                        then(last)
                last.then_inc(s["norm_made"], 1)
                dve.wait_ge(s["norm_made"], 1)
                dve.tensor_scalar(hn[:, 0, :], x[:, 0, :], gn[:, 6, 0:1], gn[:, 7, 0:1],
                                  ALU.mult, ALU.add).then_inc(s["hn_made"], 1)

            def low(hi, lo, name, o, ready, made):
                dve.wait_ge(s[ready], 1)
                dve.scalar_tensor_tensor(out=lo[:, :, :].rearrange("p b n -> p (b n)"), in0=o[:, :],
                                         scalar=col(name), in1=hi[:, :, :].rearrange("p b n -> p (b n)").bitcast(F32),
                                         op0=ALU.add, op1=ALU.subtract).then_inc(s[made], 1)

            def low_q():
                low(q_hi, q_lo, "qb", bank[0], "q_hi_made", "q_lo_made")

            def low_k():
                low(k_hi, k_lo, "kb", bank[1], "k_hi_made", "k_lo_made")

            def save_q_bottom(p):
                dve.wait_ge(s["q_tile_made"], p + 1)
                dve.tensor_copy(qs[64:128, p, 1, :, :].rearrange("p b n -> p (b n)"),
                                bank[4 + 2 * p % 4][64:128, :]).then_inc(s["q_saved_bottom_dve"], 1)

            def save_k_bottom(p):
                dve.wait_ge(s["k_tile_made"], p + 1)
                dve.tensor_copy(ks[64:128, p, 1, :, :].rearrange("p b n -> p (b n)"),
                                bank[5 + 2 * p % 4][64:128, :]).then_inc(s["k_saved_bottom"], 1)

            def derive():
                dve.wait_ge(s["fold_saved"], 1)
                dve.tensor_tensor(PB, bank[3][:, 256:257], col("pb"), ALU.add)
                dve.tensor_tensor(T1, bank[3][:, 258:259], col("bo"), ALU.add)
                dve.tensor_tensor(BCV, col("bcv"), col("beta"), ALU.mult)
                dve.tensor_scalar(BQ2, col("bq"), SCALE2, None, ALU.mult)
                then(dve.tensor_tensor(T0, bank[3][:, 257:258], col("b_so"), ALU.add))
                dve.tensor_tensor(B1, T0, col("gamma"), ALU.mult)
                dve.tensor_tensor(B2, T1, col("l3b"), ALU.add).then_inc(s["derived_made"], 1)

            def filters():
                dve.wait_ge(s["late_in"], 16)
                dve.scalar_tensor_tensor(out=down[:, :].rearrange("p (y x) -> p y x", y=8),
                                         in0=late[:, L_DR:L_DR + 8].unsqueeze(2).broadcast_to([128, 8, S]),
                                         scalar=UP_GAIN * GAIN,
                                         in1=late[:, L_DC:L_DC + S].unsqueeze(1).broadcast_to([128, 8, S]),
                                         op0=ALU.mult, op1=ALU.mult).then_inc(s["down_saved"], 1)

            def maxima(G, u):
                nt, pp, n = u // 2, u % 2, 4 * G + u
                dve.wait_ge(s["pass1_made"], n + 1)
                dve.tensor_reduce(negmax[:, G % 2, nt, :, pp], PASS1[pp][:, :].rearrange("p (a m) -> p a m", a=2),
                                  AX.X, ALU.max, negate=True).then_inc(s["max_made"], 1)

            def halve_maxima(G):
                if G == 0:
                    dve.wait_ge(s["nm_zero"], 1)
                if G >= 2:
                    dve.wait_ge(s["nmt_made"], G - 1)
                dve.wait_ge(s["max_made"], 4 * G + 4)
                raw = negmax[:, G % 2, :, :, :].rearrange("p t o q -> p (t o q)")
                halves = nm[:, G % 2, :, :, :, :].rearrange("p t o q c -> p (t o q) c")
                then(dve.tensor_copy(halves[:, :, 0], raw))
                dve.tensor_tensor(halves[:, :, 1], raw, halves[:, :, 0].bitcast(F32),
                                  ALU.subtract).then_inc(s["nm_made"], 1)

            def invert(G):
                g = G % 2
                dve.wait_ge(s["sums_made"], G + 1)
                then(dve.reciprocal(rsum[:, g, :, :].rearrange("p t j -> p (t j)"), UBANK[g][:, N:N + NT * QUAD]))
                dve.tensor_copy(rwide[:, g, :, :, :], rsum[:, g, :, :].unsqueeze(3).broadcast_to([128, NT, QUAD, 32])
                                ).then_inc(s["inverse_made"], 1)

            def divide(G):
                b, g = G // 2, G % 2
                dve.wait_ge(s["us_saved"], G + 1)
                dve.wait_ge(s["spread_made"], G + 1)
                dve.tensor_tensor(un[:, b, g, :], us[:, b, g, :], UBANK[g][:, N:2 * N],
                                  ALU.mult).then_inc(s["un_made"], 1)

            def add_x(b):
                dve.wait_ge(s["xb_made"], 1)
                dve.wait_ge(s["proj_made"], b + 1)
                dve.tensor_tensor(x1[:, b, :], UBANK[1 - b][:, 0:N], xb[:, b, :], ALU.add).then_inc(s["x1_made"], 1)

            def save_k1(b):
                dve.wait_ge(s["qk1_made"], b + 1)
                dve.tensor_scalar(qk1[:, b, 1, :], K0[b][64:128, 0:N], col("k1b", 128, 64), None,
                                  ALU.add).then_inc(s["k1_saved"], 1)

            def save_cqk(b):
                dve.wait_ge(s["rows_in"], 16)
                dve.wait_ge(s["cqk_made"], b + 1)
                dve.tensor_tensor(cqk[:, b, :, :], K1[b][:, :].rearrange("p (t c) -> p t c", t=NT),
                                  rows[:, :].unsqueeze(1).broadcast_to([128, NT, 2 * C]),
                                  ALU.add).then_inc(s["cqk_saved"], 1)

            def max1(b, nt):
                dve.wait_ge(s["s1_made"], NT * b + nt + 1)
                dve.tensor_reduce(red1[:, b, 0, nt:nt + 1], S1[nt][b][:, 0:N], AX.X, ALU.max,
                                  negate=True).then_inc(s["max1_made"], 1)

            def max_channels1(b):
                dve.wait_ge(s["e_made"], b + 1)
                dve.tensor_reduce(red1[:, b, 0, NT:NT + 1], K1[b][:, 0:C], AX.X, ALU.max,
                                  negate=True).then_inc(s["maxe_made"], 1)

            def invert1(b, nt):
                dve.wait_ge(s["exp1_made"], NT * b + nt + 1)
                dve.reciprocal(red1[:, b, 2, nt:nt + 1], red1[:, b, 1, nt:nt + 1]).then_inc(s["inverse1_made"], 1)

            def divide1(b, nt):
                dve.wait_ge(s["inverse1_made"], NT * b + nt + 1)
                dve.tensor_scalar(p1n[:, b, nt, :], p1[:, b, nt, :], red1[:, b, 2, nt:nt + 1], col("gamma"),
                                  ALU.mult, ALU.mult).then_inc(s["p1n_made"], 1)

            def divide_channels1(b):
                dve.wait_ge(s["expe_made"], b + 1)
                then(dve.reciprocal(red1[:, b, 2, NT:NT + 1], red1[:, b, 1, NT:NT + 1]))
                dve.tensor_scalar(pc[:, b, 1, :], pc[:, b, 0, :], red1[:, b, 2, NT:NT + 1], None,
                                  ALU.mult).then_inc(s["pc_made"], 1)

            def save_p1t(b):
                dve.wait_ge(s["p1t_made"], NT * b + 2)
                dve.tensor_copy(p1t[:, b, :, 128:256], P1[1][b][:, 0:N].rearrange("p (t n) -> p t n", t=NT)
                                ).then_inc(s["p1t_saved_dve"], 1)

            def add_x1(b):
                dve.wait_ge(s["x1b_made"], b + 1)
                dve.wait_ge(s["o1_made"], b + 1)
                dve.tensor_tensor(x2[:, b, :], K2[b][:, 0:N], x1b[:, b, :], ALU.add).then_inc(s["x2_made"], 1)
                dve.wait_ge(s["x2_made"], b + 1)

            def stats2(b, step):
                if step > 0:
                    dve.wait_ge(s["stat_step"], 3 * b + step)
                if step == 0:
                    last = dve.bn_stats(stat_raw2[:, b, :], x2[:, b, :])
                elif step == 1:
                    last = dve.bn_aggr(stat2[:, b, :], stat_raw2[:, b, :])
                elif step == 2:
                    last = dve.tensor_tensor(gn2[:, b, 0:1], stat2[:, b, 0:1], stat2[:, b, 0:1], ALU.mult)
                else:
                    last = dve.scalar_tensor_tensor(out=stat2[:, b, 1:2], in0=gn2[:, b, 0:1], scalar=EPS2,
                                                    in1=stat2[:, b, 1:2], op0=ALU.add, op1=ALU.add)
                last.then_inc(s["stat_step" if step < 3 else "stat_made"], 1)

            def norm2(b, step):
                if step == 0:
                    dve.wait_ge(s["gavg_made"], b + 2)
                else:
                    dve.wait_ge(s["norm_step"], b * NORM_STEPS + step)
                t = [gn2[:, b, i:i + 1] for i in range(8)]
                if step < NORM_STEPS:
                    group_norm(step, [K2[b][:, 0:2]], col("gn_w"), col("gn_b"), [t]).then_inc(s["norm_step"], 1)
                else:
                    dve.tensor_scalar(hn2[:, b, :], x2[:, b, :], t[6], t[7],
                                      ALU.mult, ALU.add).then_inc(s["hn2_made"], 1)

            def save_k2(b):
                dve.wait_ge(s["k2_made"], b + 1)
                dve.tensor_scalar(k2[:, b, :], K1[b][:, 0:N], col("bk"), None, ALU.add).then_inc(s["k2_saved"], 1)

            def max2(b, nt):
                dve.wait_ge(s["s2_made"], NT * b + nt + 1)
                dve.tensor_reduce(red2[:, b, 0, nt:nt + 1], S2[nt][b][:, 0:N], AX.X, ALU.max,
                                  negate=True).then_inc(s["max2_made"], 1)

            def save_p2t(b):
                dve.wait_ge(s["p2t_made"], NT * b + 2)
                dve.tensor_copy(p2t[:, b, 1, :], P2[1][b][:, 0:N]).then_inc(s["p2t_saved_dve"], 1)

            def invert2(b):
                dve.wait_ge(s["exp2_made"], NT * b + 2)
                then(dve.reciprocal(red2[:, b, 2, :], red2[:, b, 1, :]))

            def add_x2(b):
                dve.wait_ge(s["v2_saved"], b + 1)
                dve.wait_ge(s["o2_made"], b + 1)
                for nt in range(NT):
                    dve.scalar_tensor_tensor(out=x3t[:, b, nt, :], in0=K3[b][:, nt * C:(nt + 1) * C],
                                             scalar=red2[:, b, 2, nt:nt + 1], in1=vx[:, b, 1, nt, :],
                                             op0=ALU.mult, op1=ALU.add).then_inc(s["x3_made"], 1)

            def relu3(b, i):
                bands, count = part3(b, i)
                dve.wait_ge(s["sloped_made"], count)
                dve.tensor_tensor(z[:, b, bands, :].rearrange("p t c -> p (t c)"),
                                  UP[b][i][:, 0:(bands.stop - bands.start) * C],
                                  sloped[:, b, bands, :].rearrange("p t c -> p (t c)"), ALU.max).then_inc(s["z_made"], 1)

            def save_y(b):
                dve.wait_ge(s["y_made"], b + 1)
                dve.tensor_copy(y[:, b, :], K2[b][:, PADTOP * S:PADTOP * S + N]).then_inc(s["y_saved"], 1)

            norm0()
            filters()
            low_q()
            low_k()
            save_q_bottom(0)
            save_k_bottom(0)
            save_q_bottom(1)
            save_k_bottom(1)
            maxima(0, 0)
            maxima(0, 1)
            save_k_bottom(2)
            maxima(0, 2)
            maxima(0, 3)
            save_k_bottom(3)
            halve_maxima(0)
            maxima(1, 0)
            maxima(1, 1)
            maxima(1, 2)
            maxima(1, 3)
            halve_maxima(1)
            derive()
            for G in range(2, GROUPS):
                maxima(G, 0)
                maxima(G, 1)
                maxima(G, 2)
                maxima(G, 3)
                invert(G - 2)
                halve_maxima(G)
                divide(G - 2)
            add_x(0)
            invert(2)
            save_k1(0)
            divide(2)
            invert(3)
            save_cqk(0)
            divide(3)
            max1(0, 0)
            max1(0, 1)
            max_channels1(0)
            add_x(1)
            invert1(0, 0)
            invert1(0, 1)
            divide1(0, 0)
            divide_channels1(0)
            divide1(0, 1)
            save_k1(1)
            save_p1t(0)
            max1(1, 0)
            max1(1, 1)
            invert1(1, 0)
            save_cqk(1)
            invert1(1, 1)
            add_x1(0)
            stats2(0, 0)
            stats2(0, 1)
            stats2(0, 2)
            stats2(0, 3)
            divide1(1, 0)
            divide1(1, 1)
            norm2(0, 0)
            norm2(0, 1)
            norm2(0, 2)
            max_channels1(1)
            norm2(0, 3)
            norm2(0, 4)
            norm2(0, 5)
            norm2(0, 6)
            norm2(0, 7)
            divide_channels1(1)
            save_k2(0)
            save_p1t(1)
            add_x1(1)
            stats2(1, 0)
            stats2(1, 1)
            stats2(1, 2)
            stats2(1, 3)
            max2(0, 0)
            max2(0, 1)
            norm2(1, 0)
            norm2(1, 1)
            norm2(1, 2)
            norm2(1, 3)
            norm2(1, 4)
            norm2(1, 5)
            norm2(1, 6)
            norm2(1, 7)
            invert2(0)
            save_p2t(0)
            save_k2(1)
            add_x2(0)
            max2(1, 0)
            max2(1, 1)
            relu3(0, 0)
            relu3(0, 1)
            save_p2t(1)
            invert2(1)
            add_x2(1)
            relu3(1, 0)
            relu3(1, 1)
            relu3(1, 2)
            relu3(1, 3)
            save_y(0)
            save_y(1)


def toeplitz(f, offset, rows, row_step, cols, col_step):
    import numpy as np
    at = offset + row_step * np.arange(rows)[:, None] + col_step * np.arange(cols)[None, :]
    padded = np.concatenate([f, np.zeros(1, f.dtype)])
    return padded[np.where((at >= 0) & (at < len(f)), at, len(f))]


def kernel(**inputs):
    import numpy as np
    import concourse.bacc as bacc
    from concourse.bass_utils import run_bass_kernel_spmd

    a = {k: np.ascontiguousarray(v) for k, v in inputs.items()}

    def constant(shape):
        return np.zeros(shape, np.float32)

    def quads(rows):
        laid = np.zeros((QUAD, 32, 2, rows.shape[1]), np.float32)
        laid[:, 0:HD] = rows.reshape(2, QUAD, HD, -1).transpose(1, 2, 0, 3)
        return laid.reshape(128, 2, -1)

    cols = constant((128, len(COLS)))

    def put(name, v, rows=slice(0, 128)):
        cols[rows, COL[name]] = v

    put("norm_w", a["L0_conv_norm_w"])
    put("norm_b", a["L0_conv_norm_b"])
    for i, name in enumerate(("qb", "kb")):
        put(name, a["L0_conv_qkv_b"][i * C:(i + 1) * C])
    cols[:, [COL["vb0"], COL["vb1"]]] = quads(a["L0_conv_qkv_b"][2 * C:, None])[:, :, 0]
    put("pb", a["L0_conv_proj_b"])
    put("gn_w", a["L2_conv_gn_gamma"])
    put("gn_b", a["L2_conv_gn_beta"])
    for name in ("bq", "bk", "bv", "bo"):
        put(name, a["L2_conv_" + name])
    put("bcv", a["L1_conv_bcv"])
    put("b_so", a["L1_conv_b_so"])
    put("gamma", a["L1_conv_gamma"][0])
    put("beta", a["L1_conv_beta"][0])
    put("l3b", a["L3_conv_bias"])
    put("q1b", a["L1_conv_bq"], slice(0, IC))
    put("k1b", a["L1_conv_bk"], slice(64, 64 + IC))

    early = constant((128, E_WIDTH))
    channel = np.arange(128)
    early[:, E_AVG:E_AVG + 128] = (channel[:, None] // 4 == channel[None, :] // 4) * 0.25
    early[:, E_ID:E_ID + 128] = np.eye(128)
    early[:, E_ID32:E_ID32 + 32] = channel[:, None] % 32 == np.arange(32)[None, :]
    early[:, E_COLS:] = cols

    sum_rows = (channel[:, None] == 32 * np.arange(QUAD)[None, :] + HD).astype(np.float32)
    inner = constant((C, 2, 64))
    inner[:, 0, 0:IC], inner[:, 1, 0:IC] = a["L1_conv_wq"].T, a["L1_conv_wk"].T
    mid = np.concatenate([quads(a["L0_conv_proj_w"].T).reshape(128, 2 * C), inner.reshape(C, C),
                          a["L1_conv_wcq"].T, a["L1_conv_wck"].T, a["L1_conv_wcv"].T, sum_rows], 1)
    small = np.concatenate([a["L1_conv_wv"], a["L1_conv_w_so"].T, a["L1_conv_bv"][:, None]], 1)
    rows = np.concatenate([a["L1_conv_bcq"], a["L1_conv_bck"]])
    up, dn = a["L3_conv_up_filter"], a["L3_conv_down_filter"]
    up_rows = np.concatenate([np.repeat(toeplitz(up, TAPS // 2 - 1 - 8 * nt, 8, -2, 4 * NEAR, 1), S, 0)
                              for nt in range(NT)], 1)
    up_cols = np.tile(toeplitz(up, TAPS // 2 - 1, S, -2, 32, 1), (8, 1))
    dn_rows = np.repeat(toeplitz(dn, 0, 4, -1, 8, 2), 32, 0)
    dn_cols = np.tile(toeplitz(dn, TAPS // 2, 32, -1, S, 2), (4, 1))
    late = np.concatenate([a["L2_conv_wq"].T, a["L2_conv_wk"].T, a["L2_conv_wv"], a["L2_conv_wo"].T,
                           up_rows, up_cols, dn_rows, dn_cols], 1)
    arrays = {
        "x": a["x"].reshape(B, C, N), "early": early, "wqkv": np.ascontiguousarray(a["L0_conv_qkv_w"].T),
        "mid": np.ascontiguousarray(mid), "small": np.ascontiguousarray(small), "rows": rows,
        "late": np.ascontiguousarray(late),
    }
    nc = bacc.Bacc("TRN2", target_bir_lowering=False, num_devices=1)
    args = [nc.dram_tensor(f"in_{n}", v.shape, F32, kind="ExternalInput").ap() for n, v in arrays.items()]
    out = nc.dram_tensor("out", (B, C, N), F32, kind="ExternalOutput").ap()
    build(nc, *args, out)
    got = run_bass_kernel_spmd(nc, [{f"in_{n}": v for n, v in arrays.items()}], core_ids=[0])
    return got.results[0]["out"].reshape(B, C, S, S)
```
